# Optimizing a Trainium2 kernel written in Bass

```python
import numpy as np
import jax
import jax.numpy as jnp

def _softmax(x, axis=-1):
    return jax.nn.softmax(x, axis=axis)

def _gelu(x):
    return jax.nn.gelu(x, approximate=True)

def _silu(x):
    return jax.nn.silu(x)

def _sigmoid(x):
    return jax.nn.sigmoid(x)

def _layernorm(x, axis=-1, eps=1e-05):
    m = jnp.mean(x, axis=axis, keepdims=True)
    v = jnp.var(x, axis=axis, keepdims=True)
    return (x - m) / jnp.sqrt(v + eps)

def _scatter_add(tgt, idx, src, axis=0):
    return tgt.at[idx].add(src)

def _segment_sum(src, seg, n):
    return jax.ops.segment_sum(src, seg, n)
kernel_name = 'mk_recurrent_d1_jaxref_r8_ce0326'

def setup_inputs(seed: int=0):
    np.random.seed(seed)
    _w = jnp.asarray

    def _L0_attn_setup():
        import jax, jax.numpy as jnp
        import numpy as np
        B, N, D, H = (4, 512, 128, 16)
        GN_EPS = 0.00064
        key = jax.random.key(seed)
        ks = jax.random.split(key, 12)
        x = jax.random.normal(ks[0], (B, N, D), jnp.float32)
        ddd = jnp.linspace(0.0, 1.0, D).reshape(1, 1, D)
        s = 1.0 / np.sqrt(D)
        w = lambda k: jax.random.normal(k, (D, D), jnp.float32) * s
        return {'x': x, 'x_r': 1.0 - ddd ** 0.2, 'x_w': 1.0 - ddd ** 0.9, 'x_k': 1.0 - ddd ** 0.7, 'x_v': 1.0 - ddd ** 0.7, 'x_a': 1.0 - ddd ** 0.9, 'x_g': 1.0 - ddd ** 0.2, 'W_r': w(ks[1]), 'W_w': w(ks[2]), 'W_k': w(ks[3]), 'W_v': w(ks[4]), 'W_a': w(ks[5]), 'W_g': w(ks[6]), 'W_out': jax.random.normal(ks[7], (D, D), jnp.float32) * s, 'b_out': jax.random.normal(ks[8], (D,), jnp.float32) * 0.01, 'gn_w': 1.0 + 0.1 * jax.random.normal(ks[9], (D,), jnp.float32), 'gn_b': 0.1 * jax.random.normal(ks[10], (D,), jnp.float32)}
    _L0_attn_in = _L0_attn_setup()

    def _L0_ffn_setup():
        import jax, jax.numpy as jnp
        import numpy as np
        B, S, H, F, E, R, TOPK = (4, 256, 128, 512, 4, 4, 2)

        def _more_forward(x, Wg, bg, W1, b1, W2, b2):
            b, s, h = x.shape
            cur = x
            for r in range(R):
                flat = cur.reshape(-1, h)
                logits = flat @ Wg[r] + bg[r]
                vals, idx = jax.lax.top_k(logits, TOPK)
                w = jax.nn.softmax(vals, axis=-1)
                cw = jnp.sum(jax.nn.one_hot(idx, E, dtype=flat.dtype) * w[..., None], axis=1)
                hmid = jax.nn.gelu(jnp.einsum('nh,ehf->enf', flat, W1) + b1[:, None, :])
                y = jnp.einsum('enf,efh->enh', hmid, W2) + b2[:, None, :]
                out = jnp.einsum('ne,enh->nh', cw, y)
                cur = cur + out.reshape(b, s, h)
            return cur
        key = jax.random.key(seed)
        ks = jax.random.split(key, 8)
        scale = 0.02
        return {'x': jax.random.normal(ks[0], (B, S, H), dtype=jnp.float32), 'Wg': jax.random.normal(ks[1], (R, H, E), dtype=jnp.float32) * scale, 'bg': jnp.zeros((R, E), dtype=jnp.float32), 'W1': jax.random.normal(ks[2], (E, H, F), dtype=jnp.float32) * scale, 'b1': jnp.zeros((E, F), dtype=jnp.float32), 'W2': jax.random.normal(ks[3], (E, F, H), dtype=jnp.float32) * scale, 'b2': jnp.zeros((E, H), dtype=jnp.float32)}
    _L0_ffn_in = _L0_ffn_setup()
    _d = {'L0_attn_x': _L0_attn_in['x'], 'L0_attn_x_r': _L0_attn_in['x_r'], 'L0_attn_x_w': _L0_attn_in['x_w'], 'L0_attn_x_k': _L0_attn_in['x_k'], 'L0_attn_x_v': _L0_attn_in['x_v'], 'L0_attn_x_a': _L0_attn_in['x_a'], 'L0_attn_x_g': _L0_attn_in['x_g'], 'L0_attn_W_r': _L0_attn_in['W_r'], 'L0_attn_W_w': _L0_attn_in['W_w'], 'L0_attn_W_k': _L0_attn_in['W_k'], 'L0_attn_W_v': _L0_attn_in['W_v'], 'L0_attn_W_a': _L0_attn_in['W_a'], 'L0_attn_W_g': _L0_attn_in['W_g'], 'L0_attn_W_out': _L0_attn_in['W_out'], 'L0_attn_b_out': _L0_attn_in['b_out'], 'L0_attn_gn_w': _L0_attn_in['gn_w'], 'L0_attn_gn_b': _L0_attn_in['gn_b'], 'L0_ffn_Wg': _L0_ffn_in['Wg'], 'L0_ffn_bg': _L0_ffn_in['bg'], 'L0_ffn_W1': _L0_ffn_in['W1'], 'L0_ffn_b1': _L0_ffn_in['b1'], 'L0_ffn_W2': _L0_ffn_in['W2'], 'L0_ffn_b2': _L0_ffn_in['b2']}
    _x0 = _d['L0_attn_x']
    _d['L0_attn_x'] = jax.random.normal(jax.random.fold_in(jax.random.key(seed), 1), (16, 256, 128), dtype=_x0.dtype)
    del _x0
    return _d

def reference(L0_attn_x, L0_attn_x_r, L0_attn_x_w, L0_attn_x_k, L0_attn_x_v, L0_attn_x_a, L0_attn_x_g, L0_attn_W_r, L0_attn_W_w, L0_attn_W_k, L0_attn_W_v, L0_attn_W_a, L0_attn_W_g, L0_attn_W_out, L0_attn_b_out, L0_attn_gn_w, L0_attn_gn_b, L0_ffn_Wg, L0_ffn_bg, L0_ffn_W1, L0_ffn_b1, L0_ffn_W2, L0_ffn_b2):

    def _L0_attn_ref(x, x_r, x_w, x_k, x_v, x_a, x_g, W_r, W_w, W_k, W_v, W_a, W_g, W_out, b_out, gn_w, gn_b):
        import jax, jax.numpy as jnp
        import numpy as np
        B, N, D, H = (4, 512, 128, 16)
        GN_EPS = 0.00064
        b, n, d = x.shape
        prev = jnp.concatenate([jnp.zeros_like(x[:, :1]), x[:, :-1]], axis=1)
        xx = prev - x
        lin = lambda mix, W: (x + xx * mix) @ W.T
        r = jax.nn.sigmoid(lin(x_r, W_r))
        decay = jnp.exp(-jax.nn.softplus(lin(x_w, W_w)))
        k = jnp.tanh(lin(x_k, W_k))
        v = lin(x_v, W_v)
        alpha = jax.nn.sigmoid(lin(x_a, W_a))
        g = jax.nn.sigmoid(lin(x_g, W_g))
        u = alpha * k * v

        def step(state, inp):
            d_t, u_t, r_t = inp
            state = state * d_t + u_t
            return (state, r_t * state)
        inputs_tm = (jnp.swapaxes(decay, 0, 1), jnp.swapaxes(u, 0, 1), jnp.swapaxes(r, 0, 1))
        state0 = jnp.zeros((b, d), x.dtype)
        _, mixed_tm = jax.lax.scan(step, state0, inputs_tm)
        mixed = jnp.swapaxes(mixed_tm, 0, 1)
        m = mixed.reshape(b * n, H, d // H)
        mu = m.mean(-1, keepdims=True)
        var = ((m - mu) ** 2).mean(-1, keepdims=True)
        mn = ((m - mu) / jnp.sqrt(var + GN_EPS)).reshape(b, n, d)
        mn = mn * gn_w + gn_b
        return mn * g @ W_out.T + b_out

    def _L0_ffn_ref(x, Wg, bg, W1, b1, W2, b2):
        import jax, jax.numpy as jnp
        import numpy as np
        B, S, H, F, E, R, TOPK = (4, 256, 128, 512, 4, 4, 2)

        def _more_forward(x, Wg, bg, W1, b1, W2, b2):
            b, s, h = x.shape
            cur = x
            for r in range(R):
                flat = cur.reshape(-1, h)
                logits = flat @ Wg[r] + bg[r]
                vals, idx = jax.lax.top_k(logits, TOPK)
                w = jax.nn.softmax(vals, axis=-1)
                cw = jnp.sum(jax.nn.one_hot(idx, E, dtype=flat.dtype) * w[..., None], axis=1)
                hmid = jax.nn.gelu(jnp.einsum('nh,ehf->enf', flat, W1) + b1[:, None, :])
                y = jnp.einsum('enf,efh->enh', hmid, W2) + b2[:, None, :]
                out = jnp.einsum('ne,enh->nh', cw, y)
                cur = cur + out.reshape(b, s, h)
            return cur
        return _more_forward(x, Wg, bg, W1, b1, W2, b2)
    x = L0_attn_x
    xn = _layernorm(x, axis=-1)
    s = _L0_attn_ref(xn, L0_attn_x_r, L0_attn_x_w, L0_attn_x_k, L0_attn_x_v, L0_attn_x_a, L0_attn_x_g, L0_attn_W_r, L0_attn_W_w, L0_attn_W_k, L0_attn_W_v, L0_attn_W_a, L0_attn_W_g, L0_attn_W_out, L0_attn_b_out, L0_attn_gn_w, L0_attn_gn_b)
    g = _silu(_L0_ffn_ref(xn, L0_ffn_Wg, L0_ffn_bg, L0_ffn_W1, L0_ffn_b1, L0_ffn_W2, L0_ffn_b2))
    x = x + s * g
    return x

_drawn_inputs = setup_inputs


def setup_inputs(seed=0):
    import zlib

    import numpy as np

    out = dict(_drawn_inputs(seed))
    spreads = {'L0_ffn_bg': (0.0, 0.379), 'L0_ffn_b1': (0.0, 0.496), 'L0_ffn_b2': (0.0, 0.1)}
    factors = {'L0_attn_b_out': 8.0}
    for name, (base, spread) in spreads.items():
        noise = np.random.default_rng([zlib.crc32(name.encode()), seed]).standard_normal(out[name].shape)
        drawn = base * np.exp(spread * noise) if base else spread * noise
        out[name] = jnp.asarray(drawn.astype(out[name].dtype))
    for name, factor in factors.items():
        out[name] = (out[name] * factor).astype(out[name].dtype)
    return out
```

```python
import numpy as np
import concourse.bass as bass
from concourse import mybir
from contextlib import ExitStack

D = 128
SEQS, LEN = 16, 256
TOK = SEQS * LEN
E, F, R = 4, 512, 4
FT = F // D
BLK = 512
NB = TOK // BLK
TPB = BLK // D
NT = TOK // D
TURNS = R * NB
STEPS = TURNS * E
PASSES = TURNS // 2
GRP, GW = 16, 8
LN_EPS = 1e-5
GN_EPS = 0.00064
RSQRT_SEED = float(0x5F3759DF)
DMA = 16
P_R, P_W, P_K, P_V, P_A, P_G = range(6)
assert PASSES == SEQS and BLK == 2 * LEN


def mixer_gated_experts(nc, x, proj_t, mixes, wout_t, chan_vecs, wg, bg, w1, b1, w2, b2, cw_scratch, out):
    f32 = mybir.dt.float32
    f32r = mybir.dt.float32r
    i32 = mybir.dt.int32
    ALU = mybir.AluOpType
    ACT = mybir.ActivationFunctionType
    AX = mybir.AxisListType
    ds = bass.ds

    with ExitStack() as ctx:
        def sb(name, shape, dt=f32):
            return ctx.enter_context(nc.sbuf_tensor(name, shape, dt))

        def bank(name):
            return ctx.enter_context(nc.psum_tensor(name, [128, 512], f32))

        def sem(name):
            return ctx.enter_context(nc.semaphore(name))

        x_tok = sb("x_tok", [128, NT, D])
        xn_t = sb("xn_t", [128, SEQS, LEN + 1])
        cur = sb("cur", [128, TOK])
        s_t = sb("s_t", [128, TOK])
        w1_hi, w1_lo = sb("w1_hi", [128, E, F], f32r), sb("w1_lo", [128, E, F], f32r)
        w2_hi, w2_lo = sb("w2_hi", [128, E * FT, D], f32r), sb("w2_lo", [128, E * FT, D], f32r)
        pj_hi, pj_lo = sb("pj_hi", [128, 6, 2, D], f32r), sb("pj_lo", [128, 6, 2, D], f32r)
        wo_hi, wo_lo = sb("wo_hi", [128, D], f32r), sb("wo_lo", [128, D], f32r)
        wg_hi, wg_lo = sb("wg_hi", [128, R * E], f32r), sb("wg_lo", [128, R * E], f32r)
        b1_c = sb("b1_c", [128, E * FT])
        b2_c = sb("b2_c", [128, E])
        bg_b = sb("bg_b", [128, R * E])
        vec = sb("vec", [128, 3])
        gnw4, gnb2 = sb("gnw4", [128, 1]), sb("gnb2", [128, 1])
        mix = sb("mix", [128, 6])
        one_mix = sb("one_mix", [128, 6])
        ident = sb("ident", [128, 128])
        before = sb("before", [128, E, E])
        cur_hi, cur_lo = sb("cur_hi", [128, 2, BLK], f32r), sb("cur_lo", [128, 2, BLK], f32r)
        g = sb("g", [128, 2, FT * BLK])
        g_hi, g_lo = sb("g_hi", [128, 2, FT * BLK], f32r), sb("g_lo", [128, 2, FT * BLK], f32r)
        tmp = sb("tmp", [128, 2, BLK])
        cw_b = sb("cw_b", [128, 2, 128 * TPB * E])
        lg = sb("lg", [128, TPB * E])
        ge, gt = sb("ge", [128, TPB, E, E]), sb("gt", [128, TPB, E, E])
        rank = sb("rank", [128, TPB * E])
        half_sel = sb("half_sel", [128, TPB * E])
        half_l = sb("half_l", [128, TPB * E])
        half_sum = sb("half_sum", [128, TPB])
        lg_d = sb("lg_d", [128, TPB * E])
        lg_th = sb("lg_th", [128, TPB * E])
        cw = sb("cw", [128, 2, TPB * E])
        xs_hi, xs_lo = sb("xs_hi", [128, LEN + 1], f32r), sb("xs_lo", [128, LEN + 1], f32r)
        rw, ag, kv = sb("rw", [128, 2, LEN]), sb("ag", [128, 2, LEN]), sb("kv", [128, 2, LEN])
        uk, u, dec = sb("uk", [128, LEN]), sb("u", [128, LEN]), sb("dec", [128, LEN])
        st, mixed = sb("st", [128, LEN]), sb("mixed", [128, LEN])
        gsum, gvar = sb("gsum", [128, 2 * GRP]), sb("gvar", [128, 2 * GRP])
        cen, sq = sb("cen", [128, 2 * D]), sb("sq", [128, 2 * D])
        y0, y1, yt = sb("y0", [128, 2 * GRP]), sb("y1", [128, 2 * GRP]), sb("yt", [128, 2 * GRP])
        mn = sb("mn", [128, 2 * D])
        gn, gated = sb("gn", [128, LEN]), sb("gated", [128, LEN])
        go_hi, go_lo = sb("go_hi", [128, LEN], f32r), sb("go_lo", [128, LEN], f32r)
        ln = cw_b[:, 1, :]
        stats = ln[:, 0:NT * 6].rearrange("p (t c) -> p t c", c=6)
        mv = ln[:, NT * 6:NT * 8].rearrange("p (t c) -> p t c", c=2)
        veps, sdev, rstd = (ln[:, NT * n:NT * (n + 1)] for n in (8, 9, 10))
        w1_raw = g[:, 0, :].rearrange("p (e f) -> p e f", e=E)
        w2_raw = g[:, 1, :].rearrange("p (t h) -> p t h", h=D)
        proj_raw = s_t[:, 0:6 * D].rearrange("p (k j) -> p k j", k=6)
        pj_f32 = s_t[:, 6 * D:18 * D].rearrange("p (k two j) -> p k two j", k=6, two=2)
        wo_raw = s_t[:, 18 * D:19 * D]
        wg_raw = s_t[:, 19 * D:19 * D + R * E]

        hb = [bank(f"h_bank{i}") for i in range(FT)]
        yb = [bank(f"y_bank{i}") for i in range(2)]
        rb = bank("r_bank")
        pb = bank("p_bank")

        x_loaded = [sem(f"x_loaded{c}") for c in range(NB)]
        w1_loaded, w2_loaded, small_loaded = sem("w1_loaded"), sem("w2_loaded"), sem("small_loaded")
        ident_made = sem("ident_made")
        folded = sem("folded")
        hi_split, lo_split = sem("hi_split"), sem("lo_split")
        var_ready, sdev_ready, xn_ready = sem("var_ready"), sem("sdev_ready"), sem("xn_ready")
        xn_turned, xn_stored = sem("xn_turned"), sem("xn_stored")
        cur_ready = sem("cur_ready")
        cur_split = sem("cur_split")
        up_done = sem("up_done")
        gelu_done = sem("gelu_done")
        g_hi_done = sem("g_hi_done")
        g_lo_dve, g_lo_pool = sem("g_lo_dve"), sem("g_lo_pool")
        down_done = sem("down_done")
        combined = sem("combined")
        r_full, r_empty = sem("r_full"), sem("r_empty")
        p_full, p_empty = sem("p_full"), sem("p_empty")
        lgd_ready, lgth_ready = sem("lgd_ready"), sem("lgth_ready")
        cw_ready, cw_saved = sem("cw_ready"), sem("cw_saved")
        cwb_ready = [sem(f"cwb_ready{q}") for q in range(2)]
        xs_ready = sem("xs_ready")
        m_ready, mn_ready, go_ready = sem("m_ready"), sem("mn_ready"), sem("go_ready")
        dve_step = sem("dve_step")
        th_ready, z_ready, z_turned, o_ready = sem("th_ready"), sem("z_ready"), sem("z_turned"), sem("o_ready")
        stored = [sem(f"stored{q}") for q in range(2)]

        def as_f32(ap):
            return ap.bitcast(f32)

        SMALL = 8
        block = ctx.enter_context(nc.Block())

        @block.sync
        def _(sp):
            for c in range(NB):
                sp.dma_start(x_tok[:, c * TPB:(c + 1) * TPB, :],
                             x[c * BLK:(c + 1) * BLK, :].rearrange("(t p) d -> p t d", p=128)).then_inc(x_loaded[c], DMA)

            def spread_gates(k, q):
                sp.wait_ge(cw_ready, k + 1)
                sp.dma_start(cw_scratch[q], cw[:, q, :]).then_inc(cw_saved, DMA)
                sp.wait_ge(cw_saved, DMA * (k + 1))
                sp.dma_start(cw_b[:, q, :],
                             cw_scratch[q].rearrange("p c -> (p c)").partition_broadcast(128)).then_inc(cwb_ready[q], DMA)

            spread_gates(0, 0)
            with sp.Fori(0, PASSES - 1) as i:
                spread_gates(2 * i + 1, 1)
                spread_gates(2 * i + 2, 0)
            spread_gates(TURNS - 1, 1)

            def store(b_off, q, ready):
                sp.wait_ge(o_ready, ready)
                sp.dma_start(out[ds(b_off, BLK), :].rearrange("(t p) d -> p t d", p=128),
                             g[:, 1, 1024 + q * BLK:1024 + (q + 1) * BLK].rearrange("p (t d) -> p t d", t=TPB)
                             ).then_inc(stored[q], DMA)

            with sp.Fori(0, NB // 2) as j:
                row, even, odd = sp.snap(j * (2 * BLK)), sp.snap(2 * j + 1), sp.snap(2 * j + 2)
                store(row, 0, even)
                store(row + BLK, 1, odd)
            for q in range(2):
                sp.wait_ge(stored[q], DMA * (NB // 2))

        @block.gpsimd
        def _(pool):
            pool.memset(ident[:, :], 0.0).then_inc(ident_made, 1)
            pool.memset(before[:, :, :], 1.0).then_inc(ident_made, 1)
            pool.memset(xn_t[:, :, 0:1], 0.0).then_inc(ident_made, 1)
            pool.wait_ge(ident_made, 3)
            pool.affine_select(out=ident[:, :], in_=ident[:, :], compare_op=ALU.not_equal, fill=1.0,
                               base=0, pattern=[[-1, 128]], channel_multiplier=1).then_inc(ident_made, 1)
            pool.affine_select(out=before[:, :, :], in_=before[:, :, :], compare_op=ALU.is_gt, fill=0.0,
                               base=0, pattern=[[1, E], [-1, E]], channel_multiplier=0).then_inc(ident_made, 1)

            pool.wait_ge(small_loaded, DMA * SMALL)
            pool.tensor_scalar(one_mix[:, :], mix[:, :], -1.0, 1.0, ALU.mult, ALU.add).then_inc(folded, 1)
            pool.wait_ge(folded, 1)
            for k in range(6):
                for two, m in ((0, one_mix), (1, mix)):
                    pool.tensor_scalar(pj_f32[:, k, two, :], proj_raw[:, k, :], m[:, k:k + 1], 1.0,
                                       ALU.mult, ALU.mult).then_inc(folded, 1)
            for c in range(NB):
                pool.wait_ge(xn_stored, c + 1)
                pool.tensor_copy(cur[:, c * BLK:(c + 1) * BLK].rearrange("p (b t) -> p b t", b=2),
                                 xn_t[:, 2 * c:2 * c + 2, 1:LEN + 1]).then_inc(cur_ready, 4)

            def g_lo_half(s1, gb):
                pool.wait_ge(g_hi_done, 2 * s1 + 2)
                h = slice(FT * BLK // 2, FT * BLK)
                nc.gpsimd.tensor_tensor(g_lo[:, gb, h], g[:, gb, h], as_f32(g_hi[:, gb, h]),
                                        ALU.subtract).then_inc(g_lo_pool, 1)

            def one_pass(i, last):
                for t in range(8):
                    s = 8 * i + t
                    if not (last and t == 7):
                        g_lo_half(s + 1, (t + 1) % 2)
                    pool.wait_ge(combined, s + 3)
                    pool.wait_ge(cur_ready, 4 * NB + s)
                    c = cur[:, ds((s // E % NB) * BLK, BLK)]
                    nc.gpsimd.tensor_tensor(c, c, tmp[:, t % 2, :], ALU.add).then_inc(cur_ready, 1)

            g_lo_half(0, 0)
            with pool.Fori(0, PASSES - 1) as i:
                one_pass(i, False)
            one_pass(PASSES - 1, True)

        @block.scalar
        def _(act):
            act.dma_start(w1_raw, w1.rearrange("e h f -> h e f")).then_inc(w1_loaded, DMA)
            act.dma_start(mix[:, :], mixes).then_inc(small_loaded, DMA)
            act.dma_start(proj_raw, proj_t.rearrange("d (k j) -> d k j", k=6)).then_inc(small_loaded, DMA)
            act.dma_start(wo_raw, wout_t).then_inc(small_loaded, DMA)
            act.dma_start(vec[:, :], chan_vecs).then_inc(small_loaded, DMA)
            act.dma_start(wg_raw, wg).then_inc(small_loaded, DMA)
            act.dma_start(bg_b[:, :], bg.partition_broadcast(128)).then_inc(small_loaded, DMA)
            act.dma_start(b1_c[:, :], b1).then_inc(small_loaded, DMA)
            act.dma_start(b2_c[:, :], b2).then_inc(small_loaded, DMA)
            act.dma_start(w2_raw, w2.rearrange("e (t p) h -> p (e t) h", p=128)).then_inc(w2_loaded, DMA)

            def layer_sdev(c):
                act.wait_ge(var_ready, c + 1)
                nc.scalar.activation(sdev[:, c * TPB:(c + 1) * TPB], veps[:, c * TPB:(c + 1) * TPB],
                                     ACT.Sqrt).then_inc(sdev_ready, 1)

            def store_xn(c):
                act.wait_ge(xn_turned, c + 1)
                act.wait_ge(ident_made, 3)
                nc.scalar.activation(xn_t[:, 2 * c:2 * c + 2, 1:LEN + 1],
                                     yb[c % 2][:, :].rearrange("p (b t) -> p b t", b=2), ACT.Copy).then_inc(xn_stored, 1)

            layer_sdev(0)
            layer_sdev(1)
            act.wait_ge(w1_loaded, DMA)
            nc.scalar.activation(w1_hi[:, :, :], w1_raw, ACT.Copy).then_inc(hi_split, 1)
            store_xn(0)
            layer_sdev(2)
            act.wait_ge(w2_loaded, DMA)
            nc.scalar.activation(w2_hi[:, :, :], w2_raw, ACT.Copy).then_inc(hi_split, 1)
            act.wait_ge(small_loaded, DMA * SMALL)
            nc.scalar.activation(wg_hi[:, :], wg_raw, ACT.Copy).then_inc(hi_split, 1)
            store_xn(1)
            for c in range(3, NB):
                layer_sdev(c)
                store_xn(c - 1)
            store_xn(NB - 1)
            nc.scalar.activation(wo_hi[:, :], wo_raw, ACT.Copy).then_inc(hi_split, 1)
            act.wait_ge(folded, 13)
            nc.scalar.activation(pj_hi[:, :, :, :], pj_f32, ACT.Copy).then_inc(hi_split, 1)

            def router_tanh(k):
                act.wait_ge(lgd_ready, k + 1)
                nc.scalar.activation(lg_th[:, :], lg_d[:, :], ACT.Tanh).then_inc(lgth_ready, 1)

            def hidden(s1, e, gb, between=None):
                if isinstance(s1, int) and s1 == 0:
                    act.wait_ge(lo_split, 2)
                else:
                    act.wait_ge(down_done, s1)
                for half in range(2):
                    for ft in (2 * half, 2 * half + 1):
                        act.wait_ge(up_done, 4 * s1 + ft + 1)
                        nc.scalar.activation(g[:, gb, ft * BLK:(ft + 1) * BLK], hb[ft][:, :], ACT.Gelu_apprx_tanh,
                                             bias=b1_c[:, e * FT + ft:e * FT + ft + 1]).then_inc(gelu_done, 1)
                    act.wait_ge(gelu_done, 4 * s1 + 2 * half + 2)
                    h = slice(half * FT * BLK // 2, (half + 1) * FT * BLK // 2)
                    nc.scalar.activation(g_hi[:, gb, h], g[:, gb, h], ACT.Copy).then_inc(g_hi_done, 1)
                    if half == 0 and between is not None:
                        between()

            def one_pass(i, last):
                def take_rw():
                    act.wait_ge(p_full, 4 * i + 1)
                    nc.scalar.activation(rw[:, :, :], pb[:, :].rearrange("p (a t) -> p a t", a=2), ACT.Tanh,
                                         scale=0.5).then_inc(p_empty, 1)

                def take_ag():
                    act.wait_ge(p_full, 4 * i + 2)
                    nc.scalar.activation(ag[:, :, :], pb[:, :].rearrange("p (a t) -> p a t", a=2), ACT.Tanh,
                                         scale=0.5).then_inc(p_empty, 1)

                def take_kv():
                    act.wait_ge(p_full, 4 * i + 3)
                    nc.scalar.activation(kv[:, 0, :], pb[:, 0:LEN], ACT.Tanh)
                    nc.scalar.activation(kv[:, 1, :], pb[:, LEN:2 * LEN], ACT.Copy).then_inc(p_empty, 1)

                def take_s():
                    act.wait_ge(p_full, 4 * i + 4)
                    nc.scalar.activation(s_t[:, ds(i * LEN, LEN)], pb[:, 0:LEN], ACT.Identity,
                                         bias=vec[:, 2:3]).then_inc(p_empty, 1)

                def router_and_rw():
                    router_tanh(2 * i + 1)
                    take_rw()

                def router_next():
                    router_tanh(2 * i + 2)

                between = {1: router_and_rw, 2: take_ag, 3: take_kv, 7: take_s}
                if not last:
                    between[5] = router_next
                for t in range(8):
                    if last and t == 7:
                        take_s()
                    else:
                        hidden(8 * i + t + 1, (t + 1) % 4, (t + 1) % 2, between.get(t))

            router_tanh(0)
            hidden(0, 0, 0)
            with act.Fori(0, PASSES - 1) as i:
                one_pass(i, False)
            one_pass(PASSES - 1, True)

            def final_tanh(b, b_off, q, z_before):
                act.wait_ge(cur_ready, 4 * NB + STEPS - 4 * NB + 4 * b + 4)
                if z_before is not None:
                    act.wait_ge(z_ready, z_before)
                nc.scalar.activation(g[:, 0, q * BLK:(q + 1) * BLK], cur[:, ds(b_off, BLK)], ACT.Tanh,
                                     scale=0.5).then_inc(th_ready, 1)

            act.wait_ge(g_lo_dve, STEPS)
            act.wait_ge(g_lo_pool, STEPS)
            final_tanh(0, 0, 0, None)
            final_tanh(1, BLK, 1, None)
            with act.Fori(1, NB // 2) as j:
                final_tanh(2 * j, j * (2 * BLK), 0, 4 * j - 2)
                final_tanh(2 * j + 1, j * (2 * BLK) + BLK, 1, 4 * j)

        @block.vector
        def _(dve):
            class Own:
                base, n = 0, 0

            def link(ins):
                Own.n += 1
                ins.then_inc(dve_step, 1)
                dve.wait_ge(dve_step, Own.base + Own.n)

            def layer_stats(c):
                dve.wait_ge(x_loaded[c], DMA)
                for t in range(c * TPB, (c + 1) * TPB):
                    last = nc.vector.bn_stats(stats[:, t, :], x_tok[:, t, :])
                link(last)
                for t in range(c * TPB, (c + 1) * TPB):
                    last = nc.vector.bn_aggr(mv[:, t, :], stats[:, t, :])
                link(last)
                nc.vector.tensor_scalar(veps[:, c * TPB:(c + 1) * TPB], mv[:, c * TPB:(c + 1) * TPB, 1], LN_EPS, None,
                                        ALU.add).then_inc(var_ready, 1)

            def layer_norm(c):
                dve.wait_ge(sdev_ready, c + 1)
                link(nc.vector.reciprocal(rstd[:, c * TPB:(c + 1) * TPB], sdev[:, c * TPB:(c + 1) * TPB]))
                if c >= 2:
                    dve.wait_ge(xn_turned, c - 1)
                for t in range(TPB):
                    n = c * TPB + t
                    last = nc.vector.tensor_scalar(tmp[:, c % 2, t * D:(t + 1) * D], x_tok[:, n, :], mv[:, n, 0:1],
                                                   rstd[:, n:n + 1], ALU.subtract, ALU.mult)
                last.then_inc(xn_ready, 1)

            def split_cur(k, q, off):
                dve.wait_ge(cur_ready, 4 * (k + 1))
                c = cur[:, ds(off, BLK)]
                nc.vector.tensor_scalar(cur_hi[:, q, :], c, 1.0, None, ALU.mult).then_inc(cur_split, 1)
                dve.wait_ge(cur_split, 2 * k + 1)
                nc.vector.tensor_tensor(cur_lo[:, q, :], c, as_f32(cur_hi[:, q, :]), ALU.subtract).then_inc(cur_split, 1)

            def router_scores(k, job, rnd):
                l3 = lg[:, :].rearrange("p (t e) -> p t e", e=E)
                bg3 = bg_b[:, ds(rnd * E, E)].unsqueeze(1).to_broadcast([128, TPB, E])
                dve.wait_ge(r_full, job + 1)
                nc.vector.tensor_tensor(l3, rb[:, 0:TPB * E].rearrange("p (t e) -> p t e", e=E), bg3,
                                        ALU.add).then_inc(r_empty, 1)
                dve.wait_ge(r_empty, job + 1)
                l_row = l3.unsqueeze(3).to_broadcast([128, TPB, E, E])
                l_col = l3.unsqueeze(2).to_broadcast([128, TPB, E, E])
                nc.vector.tensor_tensor(gt[:, :, :, :], l_col, l_row, ALU.is_gt)
                link(nc.vector.tensor_tensor(ge[:, :, :, :], l_col, l_row, ALU.is_ge))
                bf = before[:, :, :].rearrange("p a b -> p (a b)").unsqueeze(1).to_broadcast([128, TPB, E * E])
                ge3 = ge[:, :, :, :].rearrange("p t a b -> p t (a b)")
                link(nc.vector.tensor_tensor(ge3, ge3, bf, ALU.mult))
                link(nc.vector.tensor_tensor(gt[:, :, :, :], gt[:, :, :, :], ge[:, :, :, :], ALU.max))
                link(nc.vector.tensor_reduce(rank[:, :], gt[:, :, :, :].rearrange("p t a b -> p (t a) b"), AX.X, ALU.add))
                link(nc.vector.tensor_scalar(half_sel[:, :], rank[:, :], 1.5, 0.5, ALU.is_lt, ALU.mult))
                link(nc.vector.tensor_tensor(half_l[:, :], half_sel[:, :], lg[:, :], ALU.mult))
                link(nc.vector.tensor_reduce(half_sum[:, :], half_l[:, :].rearrange("p (t e) -> p t e", e=E), AX.X, ALU.add))
                nc.vector.tensor_tensor(lg_d[:, :].rearrange("p (t e) -> p t e", e=E), l3,
                                        half_sum[:, :].unsqueeze(2).to_broadcast([128, TPB, E]),
                                        ALU.subtract).then_inc(lgd_ready, 1)

            def router_gates(k, q):
                dve.wait_ge(lgth_ready, k + 1)
                nc.vector.scalar_tensor_tensor(out=cw[:, q, :], in0=lg_th[:, :], scalar=1.0, in1=half_sel[:, :],
                                               op0=ALU.add, op1=ALU.mult).then_inc(cw_ready, 1)

            def g_lo_half(s1, gb):
                dve.wait_ge(g_hi_done, 2 * s1 + 1)
                h = slice(0, FT * BLK // 2)
                nc.vector.tensor_tensor(g_lo[:, gb, h], g[:, gb, h], as_f32(g_hi[:, gb, h]),
                                        ALU.subtract).then_inc(g_lo_dve, 1)

            def combine(i, t):
                s, q, e = 8 * i + t, t // 4, t % 4
                dve.wait_ge(down_done, s + 2)
                if e == 0:
                    dve.wait_ge(cwb_ready[q], DMA * (i + 1))
                dve.wait_ge(cur_ready, 4 * NB + s - 1)
                gates = cw_b[:, q, :].rearrange("p (c t e) -> p e t c", t=TPB, e=E)[:, e]
                nc.vector.scalar_tensor_tensor(out=tmp[:, t % 2, :].rearrange("p (t c) -> p t c", t=TPB),
                                               in0=yb[t % 2][:, :].rearrange("p (t c) -> p t c", t=TPB),
                                               scalar=b2_c[:, e:e + 1], in1=gates,
                                               op0=ALU.add, op1=ALU.mult).then_inc(combined, 1)

            layer_stats(0)
            layer_stats(1)
            layer_norm(0)
            layer_stats(2)
            dve.wait_ge(hi_split, 1)
            nc.vector.tensor_tensor(w1_lo[:, :, :], w1_raw, as_f32(w1_hi[:, :, :]), ALU.subtract).then_inc(lo_split, 1)
            layer_norm(1)
            dve.wait_ge(hi_split, 2)
            nc.vector.tensor_tensor(w2_lo[:, :, :], w2_raw, as_f32(w2_hi[:, :, :]), ALU.subtract).then_inc(lo_split, 1)
            dve.wait_ge(hi_split, 3)
            nc.vector.tensor_tensor(wg_lo[:, :], wg_raw, as_f32(wg_hi[:, :]), ALU.subtract).then_inc(lo_split, 1)
            for c in range(2, NB):
                if c + 1 < NB:
                    layer_stats(c + 1)
                layer_norm(c)
            nc.vector.tensor_scalar(gnw4[:, :], vec[:, 0:1], 0.25, None, ALU.mult)
            nc.vector.tensor_scalar(gnb2[:, :], vec[:, 1:2], 0.5, None, ALU.mult).then_inc(combined, 2)
            dve.wait_ge(hi_split, 4)
            nc.vector.tensor_tensor(wo_lo[:, :], wo_raw, as_f32(wo_hi[:, :]), ALU.subtract).then_inc(lo_split, 1)
            dve.wait_ge(hi_split, 5)
            nc.vector.tensor_tensor(pj_lo[:, :, :, :], pj_f32, as_f32(pj_hi[:, :, :, :]), ALU.subtract).then_inc(lo_split, 1)
            split_cur(0, 0, 0)
            dve.wait_ge(ident_made, 5)
            router_scores(0, 0, 0)
            router_gates(0, 0)
            g_lo_half(0, 0)

            LINKS = 7 * 2 + 18

            def mixer_input(i):
                xs = xn_t[:, ds(i, 1), :].rearrange("p a t -> p (a t)")
                nc.vector.tensor_scalar(xs_hi[:, :], xs, 1.0, None, ALU.mult).then_inc(xs_ready, 1)
                dve.wait_ge(xs_ready, 2 * i + 1)
                nc.vector.tensor_tensor(xs_lo[:, :], xs, as_f32(xs_hi[:, :]), ALU.subtract).then_inc(xs_ready, 1)

            def mixer_scan(i):
                dve.wait_ge(p_empty, 4 * i + 3)
                nc.vector.tensor_scalar(dec[:, :], rw[:, 1, :], -0.5, 0.5, ALU.mult, ALU.add)
                link(nc.vector.scalar_tensor_tensor(out=uk[:, :], in0=ag[:, 0, :], scalar=1.0, in1=kv[:, 0, :],
                                                    op0=ALU.add, op1=ALU.mult))
                link(nc.vector.scalar_tensor_tensor(out=u[:, :], in0=uk[:, :], scalar=0.5, in1=kv[:, 1, :],
                                                    op0=ALU.mult, op1=ALU.mult))
                link(nc.vector.tensor_tensor_scan(st[:, :], dec[:, :], u[:, :], 0.0, ALU.mult, ALU.add))
                nc.vector.scalar_tensor_tensor(out=mixed[:, :], in0=rw[:, 0, :], scalar=1.0, in1=st[:, :],
                                               op0=ALU.add, op1=ALU.mult).then_inc(m_ready, 1)

            def mixer_norm(i, job):
                dve.wait_ge(r_full, job + 1)
                m3 = rb[:, 0:2 * D].rearrange("p (g c) -> p g c", c=GW)
                link(nc.vector.tensor_reduce(gsum[:, :], m3, AX.X, ALU.add))
                nc.vector.scalar_tensor_tensor(out=cen[:, :].rearrange("p (g c) -> p g c", c=GW),
                                               in0=gsum[:, :].unsqueeze(2).to_broadcast([128, 2 * GRP, GW]),
                                               scalar=-1.0 / GW, in1=m3, op0=ALU.mult, op1=ALU.add).then_inc(r_empty, 1)
                dve.wait_ge(r_empty, job + 1)
                link(nc.vector.tensor_tensor(sq[:, :], cen[:, :], cen[:, :], ALU.mult))
                link(nc.vector.tensor_reduce(gvar[:, :], sq[:, :].rearrange("p (g c) -> p g c", c=GW), AX.X, ALU.add))
                link(nc.vector.tensor_scalar(gvar[:, :], gvar[:, :], 1.0 / (4 * GW), GN_EPS, ALU.mult, ALU.add))
                link(nc.vector.tensor_scalar(y0[:, :].bitcast(i32), gvar[:, :].bitcast(i32), -0.5, RSQRT_SEED,
                                             ALU.mult, ALU.add))
                a, b = y0, y1
                for _ in range(3):
                    link(nc.vector.tensor_tensor(yt[:, :], a[:, :], a[:, :], ALU.mult))
                    link(nc.vector.scalar_tensor_tensor(out=yt[:, :], in0=yt[:, :], scalar=-0.5, in1=gvar[:, :],
                                                        op0=ALU.mult, op1=ALU.mult))
                    link(nc.vector.scalar_tensor_tensor(out=b[:, :], in0=yt[:, :], scalar=1.5, in1=a[:, :],
                                                        op0=ALU.add, op1=ALU.mult))
                    a, b = b, a
                nc.vector.tensor_tensor(mn[:, :].rearrange("p (g c) -> p g c", c=GW),
                                        cen[:, :].rearrange("p (g c) -> p g c", c=GW),
                                        a[:, :].unsqueeze(2).to_broadcast([128, 2 * GRP, GW]),
                                        ALU.mult).then_inc(mn_ready, 1)

            def mixer_gate(i, job):
                dve.wait_ge(r_full, job + 1)
                nc.vector.tensor_scalar(gn[:, :], rb[:, 0:LEN], gnw4[:, :], gnb2[:, :], ALU.mult,
                                        ALU.add).then_inc(r_empty, 1)
                dve.wait_ge(r_empty, job + 1)
                link(nc.vector.scalar_tensor_tensor(out=gated[:, :], in0=ag[:, 1, :], scalar=1.0, in1=gn[:, :],
                                                    op0=ALU.add, op1=ALU.mult))
                nc.vector.tensor_scalar(go_hi[:, :], gated[:, :], 1.0, None, ALU.mult).then_inc(go_ready, 1)
                dve.wait_ge(go_ready, 2 * i + 1)
                nc.vector.tensor_tensor(go_lo[:, :], gated[:, :], as_f32(go_hi[:, :]), ALU.subtract).then_inc(go_ready, 1)

            def one_pass(i, last):
                Own.n = 0
                for t in range(8):
                    s = 8 * i + t
                    if t == 0:
                        split_cur(2 * i + 1, 1, (i % 4) * (2 * BLK) + BLK)
                        mixer_input(i)
                    elif t == 1:
                        router_scores(2 * i + 1, 4 * i + 1, i // 4)
                    elif t == 3:
                        if not last:
                            split_cur(2 * i + 2, 0, ((i + 1) % 4) * (2 * BLK))
                        mixer_scan(i)
                    elif t == 4:
                        mixer_norm(i, 4 * i + 2)
                    elif t == 5 and not last:
                        router_scores(2 * i + 2, 4 * i + 3, (i + 1) // 4)
                    elif t == 6:
                        mixer_gate(i, 4 * i + 4 - last)
                    if not (last and t == 7):
                        g_lo_half(s + 1, (t + 1) % 2)
                    if t == 1:
                        router_gates(2 * i + 1, 1)
                    elif t == 5 and not last:
                        router_gates(2 * i + 2, 0)
                    combine(i, t)
                if not last:
                    assert Own.n == LINKS, Own.n

            first = Own.base + Own.n
            with dve.Fori(0, PASSES - 1) as i:
                Own.base = first + LINKS * i
                one_pass(i, False)
            Own.base = first + LINKS * (PASSES - 1)
            one_pass(PASSES - 1, True)
            first = Own.base + Own.n

            def final(b, b_off, t_off, q, turned):
                th = g[:, 0, q * BLK:(q + 1) * BLK]
                z1 = g[:, 0, 1024 + q * BLK:1024 + (q + 1) * BLK]
                z = g[:, 1, q * BLK:(q + 1) * BLK]
                o = g[:, 1, 1024 + q * BLK:1024 + (q + 1) * BLK].rearrange("p (t d) -> p t d", t=TPB)
                dve.wait_ge(th_ready, b + 1)
                nc.vector.scalar_tensor_tensor(out=z1, in0=th, scalar=1.0, in1=cur[:, ds(b_off, BLK)], op0=ALU.add,
                                               op1=ALU.mult).then_inc(z_ready, 1)
                dve.wait_ge(z_ready, 2 * b + 1)
                if turned is not None:
                    dve.wait_ge(z_turned, turned)
                nc.vector.scalar_tensor_tensor(out=z, in0=z1, scalar=0.5, in1=s_t[:, ds(b_off, BLK)], op0=ALU.mult,
                                               op1=ALU.mult).then_inc(z_ready, 1)
                dve.wait_ge(z_turned, b + 1)
                if turned is not None:
                    dve.wait_ge(stored[q], turned * (DMA // 2) if q == 0 else (turned - 1) * (DMA // 2))
                nc.vector.tensor_tensor(o, yb[q][:, :].rearrange("p (t d) -> p t d", t=TPB),
                                        x_tok[:, ds(t_off, TPB), :], ALU.add).then_inc(o_ready, 1)

            dve.wait_ge(p_empty, 4 * PASSES)
            final(0, 0, 0, 0, None)
            final(1, BLK, TPB, 1, None)
            with dve.Fori(1, NB // 2) as j:
                final(2 * j, j * (2 * BLK), j * (2 * TPB), 0, 2 * j)
                final(2 * j + 1, j * (2 * BLK) + BLK, j * (2 * TPB) + TPB, 1, 2 * j + 1)

        @block.tensor
        def _(pe):
            def mm3(out_ap, w_hi, w_lo, v_hi, v_lo, start=True, stop=True):
                nc.tensor.matmul(out_ap, w_hi, v_lo, start=start, stop=False)
                nc.tensor.matmul(out_ap, w_lo, v_hi, start=False, stop=False)
                return nc.tensor.matmul(out_ap, w_hi, v_hi, start=False, stop=stop)

            pe.wait_ge(ident_made, 5)
            for c in range(NB):
                pe.wait_ge(xn_ready, c + 1)
                if c >= 2:
                    pe.wait_ge(xn_stored, c - 1)
                for t in range(TPB):
                    last = nc.tensor.transpose(yb[c % 2][:, t * D:(t + 1) * D], tmp[:, c % 2, t * D:(t + 1) * D], ident[:, :])
                    if c == 0 and t == 0:
                        last.then_inc(down_done, 1)
                last.then_inc(xn_turned, 1)

            def up(s1, e, q, split):
                first = isinstance(s1, int) and s1 == 0
                if split is not None:
                    pe.wait_ge(cur_split, split)
                for ft in range(FT):
                    if not first:
                        pe.wait_ge(gelu_done, 4 * s1 + ft - 3)
                    w = slice(ft * D, (ft + 1) * D)
                    mm3(hb[ft][:, :], w1_hi[:, e, w], w1_lo[:, e, w], cur_hi[:, q, :], cur_lo[:, q, :]).then_inc(up_done, 1)

            def down(s, e, b):
                pe.wait_ge(combined, s + 1)
                for ft in range(FT):
                    if ft % 2 == 0:
                        pe.wait_ge(g_hi_done, 2 * s + ft // 2 + 1)
                    hi = g_hi[:, b, ft * BLK:(ft + 1) * BLK]
                    nc.tensor.matmul(yb[b][:, :], w2_hi[:, e * FT + ft, :], hi, start=(ft == 0), stop=False)
                    nc.tensor.matmul(yb[b][:, :], w2_lo[:, e * FT + ft, :], hi, start=False, stop=False)
                for ft in range(FT):
                    if ft == 0:
                        pe.wait_ge(g_lo_dve, s + 1)
                    if ft == FT // 2:
                        pe.wait_ge(g_lo_pool, s + 1)
                    last = nc.tensor.matmul(yb[b][:, :], w2_hi[:, e * FT + ft, :], g_lo[:, b, ft * BLK:(ft + 1) * BLK],
                                            start=False, stop=(ft == FT - 1))
                last.then_inc(down_done, 1)

            def logits(k, q, job, rnd):
                pe.wait_ge(cur_split, 2 * (k + 1))
                if not (isinstance(job, int) and job == 0):
                    pe.wait_ge(r_empty, job)
                for t in range(TPB):
                    c = slice(t * D, (t + 1) * D)
                    last = mm3(rb[:, t * E:(t + 1) * E], cur_hi[:, q, c], cur_lo[:, q, c],
                               wg_hi[:, ds(rnd * E, E)], wg_lo[:, ds(rnd * E, E)])
                last.then_inc(r_full, 1)

            def project(i, job, kinds):
                if job == 0:
                    pe.wait_ge(xs_ready, 2 * i + 2)
                else:
                    pe.wait_ge(p_empty, 4 * i + job)
                for n, k in enumerate(kinds):
                    o = pb[:, n * LEN:(n + 1) * LEN]
                    mm3(o, pj_hi[:, k, 0, :], pj_lo[:, k, 0, :], xs_hi[:, 1:LEN + 1], xs_lo[:, 1:LEN + 1], stop=False)
                    last = mm3(o, pj_hi[:, k, 1, :], pj_lo[:, k, 1, :], xs_hi[:, 0:LEN], xs_lo[:, 0:LEN], start=False)
                last.then_inc(p_full, 1)

            def turn(job, src, ready, count):
                pe.wait_ge(ready, count)
                pe.wait_ge(r_empty, job)
                for t in range(2):
                    last = nc.tensor.transpose(rb[:, t * D:(t + 1) * D], src[:, t * D:(t + 1) * D], ident[:, :])
                last.then_inc(r_full, 1)

            def one_pass(i, last):
                for t in range(8):
                    if not (last and t == 7):
                        k1 = (t + 1) // 4
                        up(8 * i + t + 1, (t + 1) % 4, k1 % 2, 2 * (2 * i + k1 + 1) if (t + 1) % 4 == 0 else None)
                    down(8 * i + t, t % 4, t % 2)
                    if t == 0:
                        logits(2 * i + 1, 1, 4 * i + 1, i // 4)
                        project(i, 0, (P_R, P_W))
                    elif t == 1:
                        project(i, 1, (P_A, P_G))
                    elif t == 2:
                        project(i, 2, (P_K, P_V))
                    elif t == 3:
                        turn(4 * i + 2, mixed, m_ready, i + 1)
                    elif t == 4 and not last:
                        logits(2 * i + 2, 0, 4 * i + 3, (i + 1) // 4)
                    elif t == 5:
                        turn(4 * i + 4 - last, mn, mn_ready, i + 1)
                    elif t == 6:
                        pe.wait_ge(go_ready, 2 * i + 2)
                        pe.wait_ge(p_empty, 4 * i + 3)
                        mm3(pb[:, 0:LEN], wo_hi[:, :], wo_lo[:, :], go_hi[:, :], go_lo[:, :]).then_inc(p_full, 1)

            pe.wait_ge(lo_split, 5)
            pe.wait_ge(xn_stored, NB)
            logits(0, 0, 0, 0)
            up(0, 0, 0, 2)
            with pe.Fori(0, PASSES - 1) as i:
                one_pass(i, False)
            one_pass(PASSES - 1, True)

            def final(b, q, read):
                pe.wait_ge(z_ready, 2 * b + 2)
                if read is not None:
                    pe.wait_ge(o_ready, read)
                for t in range(TPB):
                    c = slice(q * BLK + t * D, q * BLK + (t + 1) * D)
                    last = nc.tensor.transpose(yb[q][:, t * D:(t + 1) * D], g[:, 1, c], ident[:, :])
                last.then_inc(z_turned, 1)

            pe.wait_ge(combined, 2 + STEPS)
            final(0, 0, None)
            final(1, 1, None)
            with pe.Fori(1, NB // 2) as j:
                final(2 * j, 0, 2 * j - 1)
                final(2 * j + 1, 1, 2 * j)


def kernel(**inputs):
    import concourse.bacc as _bacc
    from concourse.bass_utils import run_bass_kernel_spmd as _run

    a = {k: np.asarray(v) for k, v in inputs.items()}
    kinds = "rwkvag"
    host = {
        "x": a["L0_attn_x"].reshape(TOK, D),
        "proj_t": np.concatenate([a[f"L0_attn_W_{k}"].T for k in kinds], axis=1),
        "mixes": np.stack([a[f"L0_attn_x_{k}"].reshape(D) for k in kinds], axis=1),
        "wout_t": a["L0_attn_W_out"].T,
        "chan_vecs": np.stack([a["L0_attn_gn_w"], a["L0_attn_gn_b"], a["L0_attn_b_out"]], axis=1),
        "wg": a["L0_ffn_Wg"].transpose(1, 0, 2).reshape(D, R * E),
        "bg": a["L0_ffn_bg"].reshape(R * E),
        "w1": a["L0_ffn_W1"],
        "b1": a["L0_ffn_b1"].reshape(E * FT, D).T,
        "w2": a["L0_ffn_W2"],
        "b2": a["L0_ffn_b2"].T,
    }
    nc = _bacc.Bacc("TRN2", target_bir_lowering=False, num_devices=1)
    arrays, args = {}, []
    for name, v in host.items():
        v = np.ascontiguousarray(v)
        arrays[f"in_{name}"] = v
        args.append(nc.dram_tensor(f"in_{name}", v.shape, mybir.dt.from_np(v.dtype), kind="ExternalInput").ap())
    scratch = nc.dram_tensor("cw_scratch", (2, 128, TPB * E), mybir.dt.float32, kind="Internal").ap()
    out = nc.dram_tensor("out_0", (TOK, D), mybir.dt.float32, kind="ExternalOutput").ap()
    mixer_gated_experts(nc, *args, scratch, out)
    r = _run(nc, [arrays], core_ids=[0])
    return r.results[0]["out_0"].reshape(SEQS, LEN, D)
```

```python
import numpy as np
import concourse.bass as bass
from concourse import mybir
from contextlib import ExitStack

D = 128
SEQS, LEN = 16, 256
TOK = SEQS * LEN
E, F, R = 4, 512, 4
FT = F // D
BLK = 512
NB = TOK // BLK
TPB = BLK // D
NT = TOK // D
TURNS = R * NB
STEPS = TURNS * E
PASSES = TURNS // 2
GRP, GW = 16, 8
LN_EPS = 1e-5
GN_EPS = 0.00064
RSQRT_SEED = float(0x5F3759DF)
SPLIT_PASSES = 3
TAIL_PASS = PASSES - 3
DMA = 16
P_R, P_W, P_K, P_V, P_A, P_G = range(6)
assert PASSES == SEQS and BLK == 2 * LEN


def mixer_gated_experts(nc, x, proj_t, mixes, wout_t, chan_vecs, wg, bg, w1, b1, w2, b2, cw_scratch, out):
    f32 = mybir.dt.float32
    f32r = mybir.dt.float32r
    i32 = mybir.dt.int32
    ALU = mybir.AluOpType
    ACT = mybir.ActivationFunctionType
    AX = mybir.AxisListType
    ds = bass.ds

    with ExitStack() as ctx:
        def sb(name, shape, dt=f32):
            return ctx.enter_context(nc.sbuf_tensor(name, shape, dt))

        def bank(name):
            return ctx.enter_context(nc.psum_tensor(name, [128, 512], f32))

        def sem(name):
            return ctx.enter_context(nc.semaphore(name))

        xn_t = sb("xn_t", [128, SEQS, LEN + 1])
        cur = sb("cur", [128, TOK])
        w1_hi, w1_lo = sb("w1_hi", [128, E, F], f32r), sb("w1_lo", [128, E, F], f32r)
        w2_hi, w2_lo = sb("w2_hi", [128, E * FT, D], f32r), sb("w2_lo", [128, E * FT, D], f32r)
        pj_hi, pj_lo = sb("pj_hi", [128, 6, D], f32r), sb("pj_lo", [128, 6, D], f32r)
        wo_hi, wo_lo = sb("wo_hi", [128, D], f32r), sb("wo_lo", [128, D], f32r)
        wg_c = sb("wg_c", [128, R * E])
        b1_c = sb("b1_c", [128, E * FT])
        b2_c = sb("b2_c", [128, E])
        bg_b = sb("bg_b", [128, R * E])
        vec = sb("vec", [128, 3])
        gnw4, gnb2 = sb("gnw4", [128, 1]), sb("gnb2", [128, 1])
        mix = sb("mix", [128, 6])
        ident = sb("ident", [128, 128])
        before = sb("before", [128, E, E])
        cur_f = sb("cur_f", [128, 2, BLK])
        cur_hi, cur_lo = sb("cur_hi", [128, 2, BLK], f32r), sb("cur_lo", [128, 2, BLK], f32r)
        g = sb("g", [128, 2, FT * BLK])
        g_hi, g_lo = sb("g_hi", [128, 2, FT * BLK], f32r), sb("g_lo", [128, 2, FT * BLK], f32r)
        tmp = sb("tmp", [128, 2, BLK])
        cw_b = sb("cw_b", [128, 2, 128 * TPB * E])
        lg = sb("lg", [128, TPB * E])
        ge, gt = sb("ge", [128, TPB, E, E]), sb("gt", [128, TPB, E, E])
        rank = sb("rank", [128, TPB * E])
        half_sel = sb("half_sel", [128, TPB * E])
        half_l = sb("half_l", [128, TPB * E])
        half_sum = sb("half_sum", [128, TPB])
        lg_d = sb("lg_d", [128, TPB * E])
        lg_th = sb("lg_th", [128, TPB * E])
        cw = sb("cw", [128, 2, TPB * E])
        xx = sb("xx", [128, LEN])
        xm = sb("xm", [128, 2, LEN])
        xm_hi, xm_lo = sb("xm_hi", [128, 2, 2, LEN], f32r), sb("xm_lo", [128, 2, 2, LEN], f32r)
        rw, ag, kv = sb("rw", [128, 2, LEN]), sb("ag", [128, 2, LEN]), sb("kv", [128, 2, LEN])
        uk, u, dec = sb("uk", [128, LEN]), sb("u", [128, LEN]), sb("dec", [128, LEN])
        st, mixed = sb("st", [128, LEN]), sb("mixed", [128, LEN])
        gsum, gvar = sb("gsum", [128, 2 * GRP]), sb("gvar", [128, 2 * GRP])
        cen, sq = sb("cen", [128, 2 * D]), sb("sq", [128, 2 * D])
        y0, y1, yt = sb("y0", [128, 2 * GRP]), sb("y1", [128, 2 * GRP]), sb("yt", [128, 2 * GRP])
        mn = sb("mn", [128, 2 * D])
        gn, gated = sb("gn", [128, LEN]), sb("gated", [128, LEN])
        go_hi, go_lo = sb("go_hi", [128, LEN], f32r), sb("go_lo", [128, LEN], f32r)
        stats = sb("stats", [128, TPB, 6])
        mean, mdif, veps = (sb(n, [128, TPB]) for n in ("mean", "mdif", "veps"))
        xn_st = sb("xn_st", [128, BLK])
        th, z, o, xr = (sb(n, [128, 2, BLK]) for n in ("th", "z", "o", "xr"))
        w1_raw = g[:, 0, :].rearrange("p (e f) -> p e f", e=E)
        w2_raw = g[:, 1, :].rearrange("p (t h) -> p t h", h=D)
        proj_raw = cw_b[:, 1, 0:6 * D].rearrange("p (k j) -> p k j", k=6)
        wo_raw = cw_b[:, 1, 6 * D:7 * D]

        hb = [bank(f"h_bank{i}") for i in range(FT)]
        yb = [bank(f"y_bank{i}") for i in range(2)]
        rb = bank("r_bank")
        pb = bank("p_bank")

        x_loaded = [sem(f"x_loaded{c}") for c in range(NB)]
        w1_loaded = [sem(f"w1_loaded{e}") for e in range(E)]
        w2_loaded, small_loaded, mixw_loaded = sem("w2_loaded"), sem("small_loaded"), sem("mixw_loaded")
        made = sem("made")
        hi_split = sem("hi_split")
        lo_dve, lo_pool = sem("lo_dve"), sem("lo_pool")
        xn_ready = sem("xn_ready")
        summed = sem("summed")
        cur_split = sem("cur_split")
        up_done = sem("up_done")
        gelu_done = sem("gelu_done")
        g_hi_done = sem("g_hi_done")
        g_lo_dve, g_lo_pool = sem("g_lo_dve"), sem("g_lo_pool")
        down_done = sem("down_done")
        combined = sem("combined")
        r_full, r_empty = sem("r_full"), sem("r_empty")
        p_full, p_empty = sem("p_full"), sem("p_empty")
        lgd_ready, lgth_ready = sem("lgd_ready"), sem("lgth_ready")
        cw_ready, cw_saved = sem("cw_ready"), sem("cw_saved")
        cwb_ready = [sem(f"cwb_ready{q}") for q in range(2)]
        xm_ready = sem("xm_ready")
        m_ready, mn_ready, go_ready = sem("m_ready"), sem("mn_ready"), sem("go_ready")
        dve_step = sem("dve_step")
        th_ready, z_ready = sem("th_ready"), sem("z_ready")
        x_again = [sem(f"x_again{q}") for q in range(2)]
        stored = [sem(f"stored{q}") for q in range(2)]

        def as_f32(ap):
            return ap.bitcast(f32)

        SMALL, MIXW = 6, 2

        NORMING = ("logits_odd", "norm_even", "mixed", "logits_even", "mn", "norm_odd")
        PLAIN = ("logits_odd", "mixed", "logits_even", "mn")
        ENDING = ("logits_odd", "end_even", "mixed", "logits_even", "mn", "end_odd")
        LAST = ("logits_odd", "end_even", "mixed", "mn", "end_odd", "end_6")
        R_BEFORE = 3
        R_PLAIN = R_BEFORE + SPLIT_PASSES * len(NORMING)
        R_ENDING = R_PLAIN + (TAIL_PASS - SPLIT_PASSES) * len(PLAIN)

        def jobs_of(i, kind):
            start = {NORMING: R_BEFORE, PLAIN: R_PLAIN - SPLIT_PASSES * len(PLAIN),
                     ENDING: R_ENDING - TAIL_PASS * len(ENDING), LAST: R_ENDING - TAIL_PASS * len(ENDING)}[kind]
            width = len(PLAIN) if kind == PLAIN else len(ENDING)
            return {name: width * i + start + n for n, name in enumerate(kind)}

        def end_job(b):
            i = TAIL_PASS + b // 2
            if i < PASSES:
                return jobs_of(i, LAST if i == PASSES - 1 else ENDING)["end_odd" if b % 2 else "end_even"]
            return jobs_of(PASSES - 1, LAST)["end_6"] + b % 2

        def passes(engine, one_pass, before_kind=None):
            for kind, a, b in ((NORMING, 0, SPLIT_PASSES), (PLAIN, SPLIT_PASSES, TAIL_PASS)):
                if before_kind is not None:
                    before_kind(kind)
                with engine.Fori(a, b) as i:
                    one_pass(i, kind)
            if before_kind is not None:
                before_kind(ENDING)
            for i in range(TAIL_PASS, PASSES):
                one_pass(i, LAST if i == PASSES - 1 else ENDING)

        block = ctx.enter_context(nc.Block())

        @block.sync
        def _(sp):
            def load_x(c):
                sp.dma_start(cur[:, c * BLK:(c + 1) * BLK].rearrange("p (t d) -> p t d", t=TPB),
                             x[c * BLK:(c + 1) * BLK, :].rearrange("(t p) d -> p t d", p=128)).then_inc(x_loaded[c], DMA)

            load_x(0)
            for e in range(E):
                sp.dma_start(w1_raw[:, e, :], w1[e]).then_inc(w1_loaded[e], DMA)
            load_x(1)
            sp.dma_start(w2_raw, w2.rearrange("e (t p) h -> p (e t) h", p=128)).then_inc(w2_loaded, DMA)
            for c in range(2, NB):
                load_x(c)

            def spread_gates(k, q):
                sp.wait_ge(cw_ready, k + 1)
                sp.dma_start(cw_scratch[q], cw[:, q, :]).then_inc(cw_saved, DMA)
                sp.wait_ge(cw_saved, DMA * (k + 1))
                sp.dma_start(cw_b[:, q, :],
                             cw_scratch[q].rearrange("p c -> (p c)").partition_broadcast(128)).then_inc(cwb_ready[q], DMA)

            def load_x_again(b):
                if b >= 2:
                    sp.wait_ge(r_empty, end_job(b - 2) + 1)
                sp.dma_start(xr[:, b % 2, :].rearrange("p (t d) -> p t d", t=TPB),
                             x[b * BLK:(b + 1) * BLK, :].rearrange("(t p) d -> p t d", p=128)).then_inc(x_again[b % 2], DMA)

            def store(b):
                sp.wait_ge(r_empty, end_job(b) + 1)
                sp.dma_start(out[b * BLK:(b + 1) * BLK, :].rearrange("(t p) d -> p t d", p=128),
                             o[:, b % 2, :].rearrange("p (t d) -> p t d", t=TPB)).then_inc(stored[b % 2], DMA)

            spread_gates(0, 0)
            with sp.Fori(0, TAIL_PASS) as i:
                spread_gates(2 * i + 1, 1)
                spread_gates(2 * i + 2, 0)
            for i in range(TAIL_PASS, PASSES):
                b = 2 * (i - TAIL_PASS)
                load_x_again(b)
                load_x_again(b + 1)
                spread_gates(2 * i + 1, 1)
                store(b)
                if i < PASSES - 1:
                    spread_gates(2 * i + 2, 0)
                else:
                    load_x_again(NB - 2)
                store(b + 1)
            load_x_again(NB - 1)
            store(NB - 2)
            store(NB - 1)
            for q in range(2):
                sp.wait_ge(stored[q], DMA * (NB // 2))

        @block.gpsimd
        def _(pool):
            pool.memset(ident[:, :], 0.0).then_inc(made, 1)
            pool.memset(before[:, :, :], 1.0).then_inc(made, 1)
            pool.wait_ge(made, 2)
            pool.affine_select(out=ident[:, :], in_=ident[:, :], compare_op=ALU.not_equal, fill=1.0,
                               base=0, pattern=[[-1, 128]], channel_multiplier=1).then_inc(made, 1)
            pool.affine_select(out=before[:, :, :], in_=before[:, :, :], compare_op=ALU.is_gt, fill=0.0,
                               base=0, pattern=[[1, E], [-1, E]], channel_multiplier=0).then_inc(made, 1)
            pool.memset(xn_t[:, :, 0:1], 0.0).then_inc(summed, 2)

            for e in range(E):
                h = slice(e * FT, (e + 1) * FT)
                pool.wait_ge(hi_split, E + e + 1)
                nc.gpsimd.tensor_tensor(w2_lo[:, h, :], w2_raw[:, h, :], as_f32(w2_hi[:, h, :]),
                                        ALU.subtract).then_inc(lo_pool, 1)

            def mixer_weights():
                pool.wait_ge(hi_split, 2 * E + 2)
                nc.gpsimd.tensor_tensor(wo_lo[:, :], wo_raw, as_f32(wo_hi[:, :]), ALU.subtract).then_inc(lo_pool, 1)
                nc.gpsimd.tensor_tensor(pj_lo[:, :, :], proj_raw, as_f32(pj_hi[:, :, :]), ALU.subtract).then_inc(lo_pool, 1)

            def g_lo_half(s1, gb):
                pool.wait_ge(g_hi_done, 2 * s1 + 2)
                h = slice(FT * BLK // 2, FT * BLK)
                nc.gpsimd.tensor_tensor(g_lo[:, gb, h], g[:, gb, h], as_f32(g_hi[:, gb, h]),
                                        ALU.subtract).then_inc(g_lo_pool, 1)

            def one_pass(i, kind):
                for t in range(8):
                    s = 8 * i + t
                    if not (kind == LAST and t == 7):
                        g_lo_half(s + 1, (t + 1) % 2)
                    pool.wait_ge(combined, s + 3)
                    pool.wait_ge(summed, s + 2)
                    c = cur[:, ds((s // E % NB) * BLK, BLK)]
                    nc.gpsimd.tensor_tensor(c, c, tmp[:, t % 2, :], ALU.add).then_inc(summed, 1)

            g_lo_half(0, 0)
            mixer_weights()
            passes(pool, one_pass)

        @block.scalar
        def _(act):
            act.dma_start(wg_c[:, :], wg).then_inc(small_loaded, DMA)
            act.dma_start(bg_b[:, :], bg.partition_broadcast(128)).then_inc(small_loaded, DMA)
            act.dma_start(b1_c[:, :], b1).then_inc(small_loaded, DMA)
            act.dma_start(b2_c[:, :], b2).then_inc(small_loaded, DMA)
            act.dma_start(vec[:, :], chan_vecs).then_inc(small_loaded, DMA)
            act.dma_start(mix[:, :], mixes).then_inc(small_loaded, DMA)
            act.dma_start(proj_raw, proj_t.rearrange("d (k j) -> d k j", k=6)).then_inc(mixw_loaded, DMA)
            act.dma_start(wo_raw, wout_t).then_inc(mixw_loaded, DMA)

            for e in range(E):
                act.wait_ge(w1_loaded[e], DMA)
                nc.scalar.activation(w1_hi[:, e, :], w1_raw[:, e, :], ACT.Copy).then_inc(hi_split, 1)
            act.wait_ge(small_loaded, DMA * SMALL)

            def router_tanh(k):
                act.wait_ge(lgd_ready, k + 1)
                nc.scalar.activation(lg_th[:, :], lg_d[:, :], ACT.Tanh).then_inc(lgth_ready, 1)

            def hidden(s1, e, gb, first=None, between=None):
                if first is not None:
                    first()
                if isinstance(s1, int) and s1 == 0:
                    act.wait_ge(lo_dve, E)
                else:
                    act.wait_ge(down_done, s1)
                for half in range(2):
                    for ft in (2 * half, 2 * half + 1):
                        act.wait_ge(up_done, 4 * s1 + ft + 1)
                        nc.scalar.activation(g[:, gb, ft * BLK:(ft + 1) * BLK], hb[ft][:, :], ACT.Gelu_apprx_tanh,
                                             bias=b1_c[:, e * FT + ft:e * FT + ft + 1]).then_inc(gelu_done, 1)
                    act.wait_ge(gelu_done, 4 * s1 + 2 * half + 2)
                    h = slice(half * FT * BLK // 2, (half + 1) * FT * BLK // 2)
                    nc.scalar.activation(g_hi[:, gb, h], g[:, gb, h], ACT.Copy).then_inc(g_hi_done, 1)
                    if half == 0 and between is not None:
                        between()

            def one_pass(i, kind):
                def take_rw():
                    act.wait_ge(p_full, 4 * i + 1)
                    nc.scalar.activation(rw[:, :, :], pb[:, :].rearrange("p (a t) -> p a t", a=2), ACT.Tanh,
                                         scale=0.5).then_inc(p_empty, 1)

                def take_ag():
                    act.wait_ge(p_full, 4 * i + 2)
                    nc.scalar.activation(ag[:, :, :], pb[:, :].rearrange("p (a t) -> p a t", a=2), ACT.Tanh,
                                         scale=0.5).then_inc(p_empty, 1)

                def take_kv():
                    act.wait_ge(p_full, 4 * i + 3)
                    nc.scalar.activation(kv[:, 0, :], pb[:, 0:LEN], ACT.Tanh)
                    nc.scalar.activation(kv[:, 1, :], pb[:, LEN:2 * LEN], ACT.Copy).then_inc(p_empty, 1)

                def take_s():
                    act.wait_ge(p_full, 4 * i + 4)
                    nc.scalar.activation(xn_t[:, ds(i, 1), 1:LEN + 1].rearrange("p a t -> p (a t)"), pb[:, 0:LEN],
                                         ACT.Identity, bias=vec[:, 2:3]).then_inc(p_empty, 1)

                first = {1: take_rw, 2: take_ag, 3: take_kv, 7: take_s}
                between = {1: lambda: router_tanh(2 * i + 1)}
                if kind != LAST:
                    between[5] = lambda: router_tanh(2 * i + 2)
                if kind in (ENDING, LAST):
                    b = 2 * (i - TAIL_PASS)
                    between[0] = lambda: end_tanh(b)
                    between[4] = lambda: end_tanh(b + 1)
                if kind == LAST:
                    between[6] = lambda: end_tanh(NB - 2)
                for t in range(8):
                    if kind == LAST and t == 7:
                        take_s()
                    else:
                        hidden(8 * i + t + 1, (t + 1) % 4, (t + 1) % 2, first.get(t), between.get(t))

            def end_tanh(b):
                act.wait_ge(summed, 2 + STEPS - E * (NB - b - 1))
                if b >= 2:
                    act.wait_ge(z_ready, b - 1)
                nc.scalar.activation(th[:, b % 2, :], cur[:, b * BLK:(b + 1) * BLK], ACT.Tanh,
                                     scale=0.5).then_inc(th_ready, 1)

            router_tanh(0)
            act.wait_ge(w2_loaded, DMA)
            for e in range(E):
                h = slice(e * FT, (e + 1) * FT)
                nc.scalar.activation(w2_hi[:, h, :], w2_raw[:, h, :], ACT.Copy).then_inc(hi_split, 1)
            hidden(0, 0, 0)
            act.wait_ge(mixw_loaded, DMA * MIXW)
            nc.scalar.activation(wo_hi[:, :], wo_raw, ACT.Copy).then_inc(hi_split, 1)
            nc.scalar.activation(pj_hi[:, :, :], proj_raw, ACT.Copy).then_inc(hi_split, 1)
            act.wait_ge(lo_pool, E)
            passes(act, one_pass)
            end_tanh(NB - 1)

        @block.vector
        def _(dve):
            class Own:
                base, n = 0, 0

            def link(ins):
                Own.n += 1
                ins.then_inc(dve_step, 1)
                dve.wait_ge(dve_step, Own.base + Own.n)

            def inverse_root(v, n):
                a, b, t = y0[:, 0:n], y1[:, 0:n], yt[:, 0:n]
                link(nc.vector.tensor_scalar(a.bitcast(i32), v.bitcast(i32), -0.5, RSQRT_SEED, ALU.mult, ALU.add))
                for _ in range(3):
                    link(nc.vector.tensor_tensor(t, a, a, ALU.mult))
                    link(nc.vector.scalar_tensor_tensor(out=t, in0=t, scalar=-0.5, in1=v, op0=ALU.mult, op1=ALU.mult))
                    link(nc.vector.scalar_tensor_tensor(out=b, in0=t, scalar=1.5, in1=a, op0=ALU.add, op1=ALU.mult))
                    a, b = b, a
                return a

            def norm_block(off):
                for t in range(TPB):
                    last = nc.vector.bn_stats(stats[:, t, :], cur[:, ds(off + t * D, D)])
                link(last)
                mean_a, sq_a, mean_b, sq_b = (stats[:, :, n] for n in (1, 2, 4, 5))
                nc.vector.tensor_tensor(mean[:, :], mean_a, mean_b, ALU.add)
                link(nc.vector.tensor_tensor(mdif[:, :], mean_a, mean_b, ALU.subtract))
                nc.vector.tensor_scalar(mean[:, :], mean[:, :], 0.5, None, ALU.mult)
                nc.vector.tensor_tensor(veps[:, :], sq_a, sq_b, ALU.add)
                link(nc.vector.tensor_tensor(mdif[:, :], mdif[:, :], mdif[:, :], ALU.mult))
                link(nc.vector.tensor_scalar(veps[:, :], veps[:, :], 1.0 / D, LN_EPS, ALU.mult, ALU.add))
                link(nc.vector.scalar_tensor_tensor(out=veps[:, :], in0=mdif[:, :], scalar=0.25, in1=veps[:, :],
                                                    op0=ALU.mult, op1=ALU.add))
                rstd = inverse_root(veps[:, :], TPB)
                for t in range(TPB):
                    last = nc.vector.tensor_scalar(xn_st[:, t * D:(t + 1) * D], cur[:, ds(off + t * D, D)],
                                                   mean[:, t:t + 1], rstd[:, t:t + 1], ALU.subtract, ALU.mult)
                last.then_inc(xn_ready, 1)

            def store_block(seq, off, job):
                dve.wait_ge(r_full, job + 1)
                dve.wait_ge(summed, 2)
                xb = xn_t[:, ds(seq, 2), 1:LEN + 1]
                nc.vector.tensor_scalar(xb, rb[:, :].rearrange("p (b t) -> p b t", b=2), 1.0, None,
                                        ALU.mult).then_inc(r_empty, 1)
                dve.wait_ge(r_empty, job + 1)
                link(nc.vector.tensor_scalar(cur[:, ds(off, BLK)].rearrange("p (b t) -> p b t", b=2), xb, 1.0, None,
                                             ALU.mult))

            def split_cur(k, q, off, sums):
                if sums is not None:
                    dve.wait_ge(summed, sums)
                link(nc.vector.tensor_scalar(cur_f[:, q, :], cur[:, ds(off, BLK)], 1.0, None, ALU.mult))
                nc.vector.tensor_scalar(cur_hi[:, q, :], cur_f[:, q, :], 1.0, None, ALU.mult).then_inc(cur_split, 1)
                dve.wait_ge(cur_split, 2 * k + 1)
                nc.vector.tensor_tensor(cur_lo[:, q, :], cur_f[:, q, :], as_f32(cur_hi[:, q, :]),
                                        ALU.subtract).then_inc(cur_split, 1)

            def router_scores(k, job, rnd):
                l3 = lg[:, :].rearrange("p (t e) -> p t e", e=E)
                bg3 = bg_b[:, ds(rnd * E, E)].unsqueeze(1).to_broadcast([128, TPB, E])
                dve.wait_ge(r_full, job + 1)
                nc.vector.tensor_tensor(l3, rb[:, 0:TPB * E].rearrange("p (t e) -> p t e", e=E), bg3,
                                        ALU.add).then_inc(r_empty, 1)
                dve.wait_ge(r_empty, job + 1)
                l_row = l3.unsqueeze(3).to_broadcast([128, TPB, E, E])
                l_col = l3.unsqueeze(2).to_broadcast([128, TPB, E, E])
                nc.vector.tensor_tensor(gt[:, :, :, :], l_col, l_row, ALU.is_gt)
                link(nc.vector.tensor_tensor(ge[:, :, :, :], l_col, l_row, ALU.is_ge))
                bf = before[:, :, :].rearrange("p a b -> p (a b)").unsqueeze(1).to_broadcast([128, TPB, E * E])
                ge3 = ge[:, :, :, :].rearrange("p t a b -> p t (a b)")
                link(nc.vector.tensor_tensor(ge3, ge3, bf, ALU.mult))
                link(nc.vector.tensor_tensor(gt[:, :, :, :], gt[:, :, :, :], ge[:, :, :, :], ALU.max))
                link(nc.vector.tensor_reduce(rank[:, :], gt[:, :, :, :].rearrange("p t a b -> p (t a) b"), AX.X, ALU.add))
                link(nc.vector.tensor_scalar(half_sel[:, :], rank[:, :], 1.5, 0.5, ALU.is_lt, ALU.mult))
                link(nc.vector.tensor_tensor(half_l[:, :], half_sel[:, :], lg[:, :], ALU.mult))
                link(nc.vector.tensor_reduce(half_sum[:, :], half_l[:, :].rearrange("p (t e) -> p t e", e=E), AX.X, ALU.add))
                nc.vector.tensor_tensor(lg_d[:, :].rearrange("p (t e) -> p t e", e=E), l3,
                                        half_sum[:, :].unsqueeze(2).to_broadcast([128, TPB, E]),
                                        ALU.subtract).then_inc(lgd_ready, 1)

            def router_gates(k, q):
                dve.wait_ge(lgth_ready, k + 1)
                nc.vector.scalar_tensor_tensor(out=cw[:, q, :], in0=lg_th[:, :], scalar=1.0, in1=half_sel[:, :],
                                               op0=ALU.add, op1=ALU.mult).then_inc(cw_ready, 1)

            def g_lo_half(s1, gb):
                dve.wait_ge(g_hi_done, 2 * s1 + 1)
                h = slice(0, FT * BLK // 2)
                nc.vector.tensor_tensor(g_lo[:, gb, h], g[:, gb, h], as_f32(g_hi[:, gb, h]),
                                        ALU.subtract).then_inc(g_lo_dve, 1)

            def combine(i, t):
                s, q, e = 8 * i + t, t // 4, t % 4
                dve.wait_ge(down_done, s + 2)
                if e == 0:
                    dve.wait_ge(cwb_ready[q], DMA * (i + 1))
                dve.wait_ge(summed, s + 1)
                gates = cw_b[:, q, :].rearrange("p (c t e) -> p e t c", t=TPB, e=E)[:, e]
                nc.vector.scalar_tensor_tensor(out=tmp[:, t % 2, :].rearrange("p (t c) -> p t c", t=TPB),
                                               in0=yb[t % 2][:, :].rearrange("p (t c) -> p t c", t=TPB),
                                               scalar=b2_c[:, e:e + 1], in1=gates,
                                               op0=ALU.add, op1=ALU.mult).then_inc(combined, 1)

            def w1_part(e):
                dve.wait_ge(hi_split, e + 1)
                nc.vector.tensor_tensor(w1_lo[:, e, :], w1_raw[:, e, :], as_f32(w1_hi[:, e, :]),
                                        ALU.subtract).then_inc(lo_dve, 1)

            dve.wait_ge(x_loaded[0], DMA)
            norm_block(0)
            store_block(0, 0, 0)
            split_cur(0, 0, 0, None)
            w1_part(0)
            dve.wait_ge(small_loaded, DMA * SMALL)
            dve.wait_ge(made, 4)
            router_scores(0, 1, 0)
            router_gates(0, 0)
            for e in range(1, E):
                w1_part(e)
            nc.vector.tensor_scalar(gnw4[:, :], vec[:, 0:1], 0.25, None, ALU.mult)
            nc.vector.tensor_scalar(gnb2[:, :], vec[:, 1:2], 0.5, None, ALU.mult).then_inc(combined, 2)
            g_lo_half(0, 0)
            dve.wait_ge(x_loaded[1], DMA)
            norm_block(BLK)
            store_block(2, BLK, 2)
            for c in range(2, NB):
                dve.wait_ge(x_loaded[c], DMA)

            def mixer_input(i, job, kinds):
                xs = xn_t[:, ds(i, 1), :].rearrange("p a t -> p (a t)")
                if job == 0:
                    link(nc.vector.tensor_tensor(xx[:, :], xs[:, 0:LEN], xs[:, 1:LEN + 1], ALU.subtract))
                else:
                    dve.wait_ge(xm_ready, 6 * i + 2 * job)
                for n, k in enumerate(kinds):
                    last = nc.vector.scalar_tensor_tensor(out=xm[:, n, :], in0=xx[:, :], scalar=mix[:, k:k + 1],
                                                          in1=xs[:, 1:LEN + 1], op0=ALU.mult, op1=ALU.add)
                link(last)
                b = job % 2
                if job == 2:
                    dve.wait_ge(p_full, 4 * i + 1)
                nc.vector.tensor_scalar(xm_hi[:, b, :, :], xm[:, :, :], 1.0, None, ALU.mult).then_inc(xm_ready, 1)
                dve.wait_ge(xm_ready, 6 * i + 2 * job + 1)
                nc.vector.tensor_tensor(xm_lo[:, b, :, :], xm[:, :, :], as_f32(xm_hi[:, b, :, :]),
                                        ALU.subtract).then_inc(xm_ready, 1)

            def mixer_scan(i):
                dve.wait_ge(p_empty, 4 * i + 3)
                nc.vector.tensor_scalar(dec[:, :], rw[:, 1, :], -0.5, 0.5, ALU.mult, ALU.add)
                link(nc.vector.scalar_tensor_tensor(out=uk[:, :], in0=ag[:, 0, :], scalar=1.0, in1=kv[:, 0, :],
                                                    op0=ALU.add, op1=ALU.mult))
                link(nc.vector.scalar_tensor_tensor(out=u[:, :], in0=uk[:, :], scalar=0.5, in1=kv[:, 1, :],
                                                    op0=ALU.mult, op1=ALU.mult))
                link(nc.vector.tensor_tensor_scan(st[:, :], dec[:, :], u[:, :], 0.0, ALU.mult, ALU.add))
                nc.vector.scalar_tensor_tensor(out=mixed[:, :], in0=rw[:, 0, :], scalar=1.0, in1=st[:, :],
                                               op0=ALU.add, op1=ALU.mult).then_inc(m_ready, 1)

            def mixer_norm(i, job):
                dve.wait_ge(r_full, job + 1)
                m3 = rb[:, 0:2 * D].rearrange("p (g c) -> p g c", c=GW)
                link(nc.vector.tensor_reduce(gsum[:, :], m3, AX.X, ALU.add))
                nc.vector.scalar_tensor_tensor(out=cen[:, :].rearrange("p (g c) -> p g c", c=GW),
                                               in0=gsum[:, :].unsqueeze(2).to_broadcast([128, 2 * GRP, GW]),
                                               scalar=-1.0 / GW, in1=m3, op0=ALU.mult, op1=ALU.add).then_inc(r_empty, 1)
                dve.wait_ge(r_empty, job + 1)
                link(nc.vector.tensor_tensor(sq[:, :], cen[:, :], cen[:, :], ALU.mult))
                link(nc.vector.tensor_reduce(gvar[:, :], sq[:, :].rearrange("p (g c) -> p g c", c=GW), AX.X, ALU.add))
                link(nc.vector.tensor_scalar(gvar[:, :], gvar[:, :], 1.0 / (4 * GW), GN_EPS, ALU.mult, ALU.add))
                a = inverse_root(gvar[:, :], 2 * GRP)
                nc.vector.tensor_tensor(mn[:, :].rearrange("p (g c) -> p g c", c=GW),
                                        cen[:, :].rearrange("p (g c) -> p g c", c=GW),
                                        a.unsqueeze(2).to_broadcast([128, 2 * GRP, GW]),
                                        ALU.mult).then_inc(mn_ready, 1)

            def mixer_gate(i, job):
                dve.wait_ge(r_full, job + 1)
                nc.vector.tensor_scalar(gn[:, :], rb[:, 0:LEN], gnw4[:, :], gnb2[:, :], ALU.mult,
                                        ALU.add).then_inc(r_empty, 1)
                dve.wait_ge(r_empty, job + 1)
                link(nc.vector.scalar_tensor_tensor(out=gated[:, :], in0=ag[:, 1, :], scalar=1.0, in1=gn[:, :],
                                                    op0=ALU.add, op1=ALU.mult))
                nc.vector.tensor_scalar(go_hi[:, :], gated[:, :], 1.0, None, ALU.mult).then_inc(go_ready, 1)
                dve.wait_ge(go_ready, 2 * i + 1)
                nc.vector.tensor_tensor(go_lo[:, :], gated[:, :], as_f32(go_hi[:, :]), ALU.subtract).then_inc(go_ready, 1)

            def end_product(b):
                q = b % 2
                dve.wait_ge(th_ready, b + 1)
                link(nc.vector.scalar_tensor_tensor(out=th[:, q, :], in0=th[:, q, :], scalar=1.0,
                                                    in1=cur[:, b * BLK:(b + 1) * BLK], op0=ALU.add, op1=ALU.mult))
                nc.vector.scalar_tensor_tensor(out=z[:, q, :].rearrange("p (b t) -> p b t", b=2),
                                               in0=th[:, q, :].rearrange("p (b t) -> p b t", b=2), scalar=0.5,
                                               in1=xn_t[:, 2 * b:2 * b + 2, 1:LEN + 1], op0=ALU.mult,
                                               op1=ALU.mult).then_inc(z_ready, 1)

            def end_output(b, job):
                q = b % 2
                dve.wait_ge(r_full, job + 1)
                dve.wait_ge(x_again[q], DMA * (b // 2 + 1))
                if b >= 2:
                    dve.wait_ge(stored[q], DMA * (b // 2))
                nc.vector.tensor_tensor(o[:, q, :], rb[:, :], xr[:, q, :], ALU.add).then_inc(r_empty, 1)

            def one_pass(i, kind):
                Own.n = 0
                job = jobs_of(i, kind)
                b = 2 * (i - TAIL_PASS)
                for t in range(8):
                    s = 8 * i + t
                    if t == 0:
                        split_cur(2 * i + 1, 1, (i % 4) * (2 * BLK) + BLK, None if kind == NORMING else 8 * i - 22)
                        mixer_input(i, 0, (P_R, P_W))
                    elif t == 1:
                        router_scores(2 * i + 1, job["logits_odd"], i // 4)
                        mixer_input(i, 1, (P_A, P_G))
                        if kind in (ENDING, LAST):
                            end_product(b)
                    elif t == 2:
                        mixer_input(i, 2, (P_K, P_V))
                        if kind == NORMING:
                            norm_block(i * (2 * BLK) + 2 * BLK)
                    elif t == 3:
                        if kind == NORMING:
                            store_block(4 * i + 4, i * (2 * BLK) + 2 * BLK, job["norm_even"])
                        if kind in (ENDING, LAST):
                            end_output(b, job["end_even"])
                        mixer_scan(i)
                        if kind != LAST:
                            split_cur(2 * i + 2, 0, ((i + 1) % 4) * (2 * BLK), None if kind == NORMING else 8 * i - 18)
                    elif t == 4:
                        mixer_norm(i, job["mixed"])
                    elif t == 5:
                        if kind != LAST:
                            router_scores(2 * i + 2, job["logits_even"], (i + 1) // 4)
                        if kind in (ENDING, LAST):
                            end_product(b + 1)
                    elif t == 6:
                        mixer_gate(i, job["mn"])
                        if kind == NORMING:
                            norm_block(i * (2 * BLK) + 3 * BLK)
                    elif t == 7:
                        if kind == NORMING:
                            store_block(4 * i + 6, i * (2 * BLK) + 3 * BLK, job["norm_odd"])
                        if kind in (ENDING, LAST):
                            end_output(b + 1, job["end_odd"])
                        if kind == LAST:
                            end_product(NB - 2)
                    if not (kind == LAST and t == 7):
                        g_lo_half(s + 1, (t + 1) % 2)
                    if t == 1:
                        router_gates(2 * i + 1, 1)
                    elif t == 5 and kind != LAST:
                        router_gates(2 * i + 2, 0)
                    combine(i, t)

            ROUTER, INPUT, SCAN, NORM, GATE, SPLIT, ROOT = 7, 4, 3, 14, 1, 1, 10
            LINKS = 2 * ROUTER + INPUT + SCAN + NORM + GATE + 2 * SPLIT
            LINKS_NORMING = LINKS + 2 * (5 + ROOT + 1)

            first = Own.base + Own.n
            with dve.Fori(0, SPLIT_PASSES) as i:
                Own.base = first + LINKS_NORMING * i
                one_pass(i, NORMING)
                assert Own.n == LINKS_NORMING, Own.n
            first += LINKS_NORMING * SPLIT_PASSES
            with dve.Fori(SPLIT_PASSES, TAIL_PASS) as i:
                Own.base = first - LINKS * SPLIT_PASSES + LINKS * i
                one_pass(i, PLAIN)
                assert Own.n == LINKS, Own.n
            Own.base = first + LINKS * (TAIL_PASS - SPLIT_PASSES)
            for i in range(TAIL_PASS, PASSES):
                one_pass(i, LAST if i == PASSES - 1 else ENDING)
                Own.base, Own.n = Own.base + Own.n, 0

            end_output(NB - 2, end_job(NB - 2))
            dve.wait_ge(p_empty, 4 * PASSES)
            end_product(NB - 1)
            end_output(NB - 1, end_job(NB - 1))

        @block.tensor
        def _(pe):
            def mm3(out_ap, w_hi, w_lo, v_hi, v_lo, start=True, stop=True):
                nc.tensor.matmul(out_ap, w_hi, v_lo, start=start, stop=False)
                nc.tensor.matmul(out_ap, w_lo, v_hi, start=False, stop=False)
                return nc.tensor.matmul(out_ap, w_hi, v_hi, start=False, stop=stop)

            def turn(job, src, tiles, ready, count, first=False):
                pe.wait_ge(ready, count)
                if not first:
                    pe.wait_ge(r_empty, job)
                for t in range(tiles):
                    ins = nc.tensor.transpose(rb[:, t * D:(t + 1) * D], src[:, t * D:(t + 1) * D], ident[:, :])
                    if first and t == 0:
                        ins.then_inc(down_done, 1)
                ins.then_inc(r_full, 1)

            def up(s1, e, q, split):
                first = isinstance(s1, int) and s1 == 0
                if split is not None:
                    pe.wait_ge(cur_split, split)
                for ft in range(FT):
                    if not first:
                        pe.wait_ge(gelu_done, 4 * s1 + ft - 3)
                    w = slice(ft * D, (ft + 1) * D)
                    mm3(hb[ft][:, :], w1_hi[:, e, w], w1_lo[:, e, w], cur_hi[:, q, :], cur_lo[:, q, :]).then_inc(up_done, 1)

            def down(s, e, b):
                pe.wait_ge(combined, s + 1)
                for ft in range(FT):
                    if ft % 2 == 0:
                        pe.wait_ge(g_hi_done, 2 * s + ft // 2 + 1)
                    hi = g_hi[:, b, ft * BLK:(ft + 1) * BLK]
                    nc.tensor.matmul(yb[b][:, :], w2_hi[:, e * FT + ft, :], hi, start=(ft == 0), stop=False)
                    nc.tensor.matmul(yb[b][:, :], w2_lo[:, e * FT + ft, :], hi, start=False, stop=False)
                for ft in range(FT):
                    if ft == 0:
                        pe.wait_ge(g_lo_dve, s + 1)
                    if ft == FT // 2:
                        pe.wait_ge(g_lo_pool, s + 1)
                    last = nc.tensor.matmul(yb[b][:, :], w2_hi[:, e * FT + ft, :], g_lo[:, b, ft * BLK:(ft + 1) * BLK],
                                            start=False, stop=(ft == FT - 1))
                last.then_inc(down_done, 1)

            def logits(k, q, job, rnd):
                pe.wait_ge(cur_split, 2 * (k + 1))
                pe.wait_ge(r_empty, job)
                for t in range(TPB):
                    last = nc.tensor.matmul(rb[:, t * E:(t + 1) * E], cur_f[:, q, t * D:(t + 1) * D],
                                            wg_c[:, ds(rnd * E, E)], start=True, stop=True)
                last.then_inc(r_full, 1)

            def project(i, job, kinds):
                pe.wait_ge(xm_ready, 6 * i + 2 * job + 2)
                if job > 0:
                    pe.wait_ge(p_empty, 4 * i + job)
                for n, k in enumerate(kinds):
                    last = mm3(pb[:, n * LEN:(n + 1) * LEN], pj_hi[:, k, :], pj_lo[:, k, :],
                               xm_hi[:, job % 2, n, :], xm_lo[:, job % 2, n, :])
                last.then_inc(p_full, 1)

            def one_pass(i, kind):
                job = jobs_of(i, kind)
                b = 2 * (i - TAIL_PASS)
                for t in range(8):
                    if not (kind == LAST and t == 7):
                        k1 = (t + 1) // 4
                        up(8 * i + t + 1, (t + 1) % 4, k1 % 2, 2 * (2 * i + k1 + 1) if (t + 1) % 4 == 0 else None)
                    down(8 * i + t, t % 4, t % 2)
                    if t == 0:
                        logits(2 * i + 1, 1, job["logits_odd"], i // 4)
                        project(i, 0, (P_R, P_W))
                    elif t == 1:
                        project(i, 1, (P_A, P_G))
                    elif t == 2:
                        project(i, 2, (P_K, P_V))
                        if kind == NORMING:
                            turn(job["norm_even"], xn_st, TPB, xn_ready, 2 * i + 3)
                        if kind in (ENDING, LAST):
                            turn(job["end_even"], z[:, 0, :], TPB, z_ready, b + 1)
                    elif t == 3:
                        turn(job["mixed"], mixed, 2, m_ready, i + 1)
                    elif t == 4 and kind != LAST:
                        logits(2 * i + 2, 0, job["logits_even"], (i + 1) // 4)
                    elif t == 5:
                        turn(job["mn"], mn, 2, mn_ready, i + 1)
                    elif t == 6:
                        pe.wait_ge(go_ready, 2 * i + 2)
                        pe.wait_ge(p_empty, 4 * i + 3)
                        mm3(pb[:, 0:LEN], wo_hi[:, :], wo_lo[:, :], go_hi[:, :], go_lo[:, :]).then_inc(p_full, 1)
                        if kind == NORMING:
                            turn(job["norm_odd"], xn_st, TPB, xn_ready, 2 * i + 4)
                        if kind in (ENDING, LAST):
                            turn(job["end_odd"], z[:, 1, :], TPB, z_ready, b + 2)
                    elif t == 7 and kind == LAST:
                        turn(job["end_6"], z[:, 0, :], TPB, z_ready, NB - 1)

            pe.wait_ge(made, 4)
            turn(0, xn_st, TPB, xn_ready, 1, first=True)
            pe.wait_ge(small_loaded, DMA * SMALL)
            logits(0, 0, 1, 0)
            pe.wait_ge(lo_dve, 1)
            up(0, 0, 0, 2)
            turn(2, xn_st, TPB, xn_ready, 2)
            pe.wait_ge(lo_dve, E)
            pe.wait_ge(lo_pool, E + 2)
            passes(pe, one_pass)
            turn(end_job(NB - 1), z[:, 1, :], TPB, z_ready, NB)


def kernel(**inputs):
    import concourse.bacc as _bacc
    from concourse.bass_utils import run_bass_kernel_spmd as _run

    a = {k: np.asarray(v) for k, v in inputs.items()}
    kinds = "rwkvag"
    host = {
        "x": a["L0_attn_x"].reshape(TOK, D),
        "proj_t": np.concatenate([a[f"L0_attn_W_{k}"].T for k in kinds], axis=1),
        "mixes": np.stack([a[f"L0_attn_x_{k}"].reshape(D) for k in kinds], axis=1),
        "wout_t": a["L0_attn_W_out"].T,
        "chan_vecs": np.stack([a["L0_attn_gn_w"], a["L0_attn_gn_b"], a["L0_attn_b_out"]], axis=1),
        "wg": a["L0_ffn_Wg"].transpose(1, 0, 2).reshape(D, R * E),
        "bg": a["L0_ffn_bg"].reshape(R * E),
        "w1": a["L0_ffn_W1"],
        "b1": a["L0_ffn_b1"].reshape(E * FT, D).T,
        "w2": a["L0_ffn_W2"],
        "b2": a["L0_ffn_b2"].T,
    }
    nc = _bacc.Bacc("TRN2", target_bir_lowering=False, num_devices=1)
    arrays, args = {}, []
    for name, v in host.items():
        v = np.ascontiguousarray(v)
        arrays[f"in_{name}"] = v
        args.append(nc.dram_tensor(f"in_{name}", v.shape, mybir.dt.from_np(v.dtype), kind="ExternalInput").ap())
    scratch = nc.dram_tensor("cw_scratch", (2, 128, TPB * E), mybir.dt.float32, kind="Internal").ap()
    out = nc.dram_tensor("out_0", (TOK, D), mybir.dt.float32, kind="ExternalOutput").ap()
    mixer_gated_experts(nc, *args, scratch, out)
    r = _run(nc, [arrays], core_ids=[0])
    return r.results[0]["out_0"].reshape(SEQS, LEN, D)
```

```python
import numpy as np
import concourse.bass as bass
from concourse import mybir
from contextlib import ExitStack

D = 128
SEQS, LEN = 16, 256
TOK = SEQS * LEN
E, F, R = 4, 512, 4
FT = F // D
BLK = 512
NB = TOK // BLK
TPB = BLK // D
RP = 32
RT = BLK // RP
TURNS = R * NB
STEPS = TURNS * E
PASSES = TURNS // 2
GRP, GW = 16, 8
LN_EPS = 1e-5
GN_EPS = 0.00064
RSQRT_SEED = float(0x5F3759DF)
WARM_UP = 40
SPLIT_PASSES = 3
TAIL_PASS = PASSES - 3
DMA = 16
P_R, P_W, P_K, P_V, P_A, P_G = range(6)
assert PASSES == SEQS and BLK == 2 * LEN


def mixer_gated_experts(nc, x, proj_t, mixes, wout_t, chan_vecs, wg, bg, w1, b1, w2, b2, cw_scratch, out):
    f32 = mybir.dt.float32
    f32r = mybir.dt.float32r
    i32 = mybir.dt.int32
    ALU = mybir.AluOpType
    ACT = mybir.ActivationFunctionType
    AX = mybir.AxisListType
    ds = bass.ds

    with ExitStack() as ctx:
        def sb(name, shape, dt=f32):
            return ctx.enter_context(nc.sbuf_tensor(name, shape, dt))

        def bank(name):
            return ctx.enter_context(nc.psum_tensor(name, [128, 512], f32))

        def sem(name):
            return ctx.enter_context(nc.semaphore(name))

        xn_t = sb("xn_t", [128, SEQS, LEN + 1])
        cur = sb("cur", [128, TOK])
        w1_hi, w1_lo = sb("w1_hi", [128, E, F], f32r), sb("w1_lo", [128, E, F], f32r)
        w2_hi, w2_lo = sb("w2_hi", [128, E * FT, D], f32r), sb("w2_lo", [128, E * FT, D], f32r)
        pj_hi, pj_lo = sb("pj_hi", [128, 6, D], f32r), sb("pj_lo", [128, 6, D], f32r)
        wo_hi, wo_lo = sb("wo_hi", [128, D], f32r), sb("wo_lo", [128, D], f32r)
        wg_c = sb("wg_c", [128, R, E])
        wg_hl = sb("wg_hl", [128, R, 2 * E], f32r)
        wg_now = sb("wg_now", [128, 2, 2 * E], f32r)
        b1_c = sb("b1_c", [128, E * FT])
        b2_c = sb("b2_c", [128, E])
        bg_b = sb("bg_b", [RP, R * E])
        vec = sb("vec", [128, 3])
        gnw4, gnb2 = sb("gnw4", [128, 1]), sb("gnb2", [128, 1])
        mix = sb("mix", [128, 6])
        ident = sb("ident", [128, 128])
        cur_hi, cur_lo = sb("cur_hi", [128, 2, BLK], f32r), sb("cur_lo", [128, 2, BLK], f32r)
        g = sb("g", [128, 2, FT * BLK])
        g_hi, g_lo = sb("g_hi", [128, 2, FT * BLK], f32r), sb("g_lo", [128, 2, FT * BLK], f32r)
        tmp = sb("tmp", [128, 2, BLK])
        cw_b = sb("cw_b", [128, 2, BLK * E])
        lgt = sb("lgt", [RP, RT, RP])
        lg = sb("lg", [RP, RT * E])
        ahead = sb("ahead", [RP, RT, E, E])
        rank = sb("rank", [RP, RT * E])
        half_sel = sb("half_sel", [RP, RT * E])
        sel_l = sb("sel_l", [RP, RT * E])
        sel_sum = sb("sel_sum", [RP, RT])
        lg_d = sb("lg_d", [RP, RT * E])
        lg_th = sb("lg_th", [RP, RT * E])
        cw = sb("cw", [RP, 2, RT * E])
        xx = sb("xx", [128, LEN])
        xm = sb("xm", [128, 2, LEN])
        xm_hi, xm_lo = sb("xm_hi", [128, 2, 2, LEN], f32r), sb("xm_lo", [128, 2, 2, LEN], f32r)
        rw, ag, kv = sb("rw", [128, 2, LEN]), sb("ag", [128, 2, LEN]), sb("kv", [128, 2, LEN])
        uk, u, dec = sb("uk", [128, LEN]), sb("u", [128, LEN]), sb("dec", [128, LEN])
        st, mixed = sb("st", [128, LEN]), sb("mixed", [128, LEN])
        gsum, gvar = sb("gsum", [128, 2 * GRP]), sb("gvar", [128, 2 * GRP])
        cen, sq = sb("cen", [128, 2 * D]), sb("sq", [128, 2 * D])
        y0, y1, yt = sb("y0", [128, 2 * GRP]), sb("y1", [128, 2 * GRP]), sb("yt", [128, 2 * GRP])
        rt, mn = sb("rt", [128, 2 * GRP]), sb("mn", [128, 2 * D])
        gn, gated = sb("gn", [128, LEN]), sb("gated", [128, LEN])
        go_hi, go_lo = sb("go_hi", [128, LEN], f32r), sb("go_lo", [128, LEN], f32r)
        stats = sb("stats", [128, 2 * TPB, 6])
        mean, mdif, veps, rstd = (sb(n, [128, 2 * TPB]) for n in ("mean", "mdif", "veps", "rstd"))
        xn_st = sb("xn_st", [128, 2, BLK])
        th, z, o, xr = (sb(n, [128, 2, BLK]) for n in ("th", "z", "o", "xr"))
        w1_raw = g[:, 0, :].rearrange("p (e f) -> p e f", e=E)
        w2_raw = g[:, 1, :].rearrange("p (t h) -> p t h", h=D)
        proj_raw = cw_b[:, 1, 0:6 * D].rearrange("p (k j) -> p k j", k=6)
        wo_raw = cw_b[:, 1, 6 * D:7 * D]

        hb = [bank(f"h_bank{i}") for i in range(FT)]
        yb = [bank(f"y_bank{i}") for i in range(2)]
        rb = bank("r_bank")
        pb = bank("p_bank")

        x_loaded = [sem(f"x_loaded{c}") for c in range(NB)]
        w1_loaded = [sem(f"w1_loaded{e}") for e in range(E)]
        w2_loaded, mixw_loaded = sem("w2_loaded"), sem("mixw_loaded")
        gate_loaded, small_loaded = sem("gate_loaded"), sem("small_loaded")
        wg_split = sem("wg_split")
        made = sem("made")
        hi_split = sem("hi_split")
        lo_split = sem("lo_split")
        rstd_ready = sem("rstd_ready")
        xn_ready = sem("xn_ready")
        summed = sem("summed")
        cur_split = sem("cur_split")
        up_done = sem("up_done")
        gelu_done = sem("gelu_done")
        g_hi_done = sem("g_hi_done")
        g_lo_dve, g_lo_pool = sem("g_lo_dve"), sem("g_lo_pool")
        down_done = sem("down_done")
        combined = sem("combined")
        r_full, r_empty = sem("r_full"), sem("r_empty")
        p_full, p_empty = sem("p_full"), sem("p_empty")
        lgd_ready, lgth_ready = sem("lgd_ready"), sem("lgth_ready")
        cw_ready, cw_saved = sem("cw_ready"), sem("cw_saved")
        cwb_ready = [sem(f"cwb_ready{q}") for q in range(2)]
        xm_ready = sem("xm_ready")
        m_ready, mn_ready, go_ready = sem("m_ready"), sem("mn_ready"), sem("go_ready")
        dve_step = sem("dve_step")
        th_ready, z_ready = sem("th_ready"), sem("z_ready")
        x_again = [sem(f"x_again{q}") for q in range(2)]
        stored = [sem(f"stored{q}") for q in range(2)]

        def as_f32(ap):
            return ap.bitcast(f32)

        def norm_scale(engine, off, tiles):
            for c in tiles:
                h, t = c // TPB, c % TPB
                ins = engine.tensor_scalar(xn_st[:, h, t * D:(t + 1) * D], cur[:, off + c * D:off + (c + 1) * D],
                                           mean[:, c:c + 1], rstd[:, c:c + 1], ALU.subtract, ALU.mult)
                if t == TPB - 1:
                    ins.then_inc(xn_ready, 1)

        GATEW, SMALL, MIXW = 2, 4, 2

        NORMING = ("logits_odd", "norm_even", "mixed", "logits_even", "mn", "norm_odd")
        PLAIN = ("logits_odd", "mixed", "logits_even", "mn")
        ENDING = ("logits_odd", "end_even", "mixed", "logits_even", "mn", "end_odd")
        LAST = ("logits_odd", "end_even", "mixed", "mn", "end_odd", "end_6")
        R_BEFORE = 3
        R_PLAIN = R_BEFORE + SPLIT_PASSES * len(NORMING)
        R_ENDING = R_PLAIN + (TAIL_PASS - SPLIT_PASSES) * len(PLAIN)

        def jobs_of(i, kind):
            start = {NORMING: R_BEFORE, PLAIN: R_PLAIN - SPLIT_PASSES * len(PLAIN),
                     ENDING: R_ENDING - TAIL_PASS * len(ENDING), LAST: R_ENDING - TAIL_PASS * len(ENDING)}[kind]
            width = len(PLAIN) if kind == PLAIN else len(ENDING)
            return {name: width * i + start + n for n, name in enumerate(kind)}

        def end_job(b):
            i = TAIL_PASS + b // 2
            if i < PASSES:
                return jobs_of(i, LAST if i == PASSES - 1 else ENDING)["end_odd" if b % 2 else "end_even"]
            return jobs_of(PASSES - 1, LAST)["end_6"] + b % 2

        def passes(engine, one_pass):
            for i in range(SPLIT_PASSES):
                one_pass(i, NORMING)
            with engine.Fori(SPLIT_PASSES, TAIL_PASS) as i:
                one_pass(i, PLAIN)
            for i in range(TAIL_PASS, PASSES):
                one_pass(i, LAST if i == PASSES - 1 else ENDING)

        block = ctx.enter_context(nc.Block())

        @block.sync
        def _(sp):
            def load_x(c):
                sp.dma_start(cur[:, c * BLK:(c + 1) * BLK].rearrange("p (t d) -> p t d", t=TPB),
                             x[c * BLK:(c + 1) * BLK, :].rearrange("(t p) d -> p t d", p=128)).then_inc(x_loaded[c], DMA)

            load_x(0)
            load_x(1)
            for e in range(E):
                sp.dma_start(w1_raw[:, e, :], w1[e]).then_inc(w1_loaded[e], DMA)
            sp.dma_start(w2_raw, w2.rearrange("e (t p) h -> p (e t) h", p=128)).then_inc(w2_loaded, DMA)
            sp.dma_start(b1_c[:, :], b1).then_inc(small_loaded, DMA)
            sp.dma_start(vec[:, :], chan_vecs).then_inc(small_loaded, DMA)
            sp.dma_start(mix[:, :], mixes).then_inc(small_loaded, DMA)
            sp.dma_start(b2_c[:, :], b2).then_inc(small_loaded, DMA)
            sp.dma_start(wo_raw, wout_t).then_inc(mixw_loaded, DMA)
            sp.dma_start(proj_raw, proj_t.rearrange("d (k j) -> d k j", k=6)).then_inc(mixw_loaded, DMA)
            for c in range(2, NB):
                load_x(c)

            def spread_gates(k, q):
                sp.wait_ge(cw_ready, k + 1)
                sp.dma_start(cw_scratch[q], cw[:, q, :]).then_inc(cw_saved, DMA)
                sp.wait_ge(cw_saved, DMA * (k + 1))
                sp.dma_start(cw_b[:, q, :],
                             cw_scratch[q].rearrange("p c -> (p c)").partition_broadcast(128)).then_inc(cwb_ready[q], DMA)

            def load_x_again(b):
                if b >= 2:
                    sp.wait_ge(r_empty, end_job(b - 2) + 1)
                sp.dma_start(xr[:, b % 2, :].rearrange("p (t d) -> p t d", t=TPB),
                             x[b * BLK:(b + 1) * BLK, :].rearrange("(t p) d -> p t d", p=128)).then_inc(x_again[b % 2], DMA)

            def store(b):
                sp.wait_ge(r_empty, end_job(b) + 1)
                sp.dma_start(out[b * BLK:(b + 1) * BLK, :].rearrange("(t p) d -> p t d", p=128),
                             o[:, b % 2, :].rearrange("p (t d) -> p t d", t=TPB)).then_inc(stored[b % 2], DMA)

            spread_gates(0, 0)
            with sp.Fori(0, TAIL_PASS) as i:
                spread_gates(2 * i + 1, 1)
                spread_gates(2 * i + 2, 0)
            for i in range(TAIL_PASS, PASSES):
                b = 2 * (i - TAIL_PASS)
                load_x_again(b)
                load_x_again(b + 1)
                spread_gates(2 * i + 1, 1)
                store(b)
                if i < PASSES - 1:
                    spread_gates(2 * i + 2, 0)
                else:
                    load_x_again(NB - 2)
                store(b + 1)
            load_x_again(NB - 1)
            store(NB - 2)
            store(NB - 1)
            for q in range(2):
                sp.wait_ge(stored[q], DMA * (NB // 2))

        @block.gpsimd
        def _(pool):
            pool.memset(ident[:, :], 0.0).then_inc(made, 1)
            pool.memset(ahead[:, :, :, :], 0.0).then_inc(made, 1)
            pool.wait_ge(made, 2)
            pool.affine_select(out=ident[:, :], in_=ident[:, :], compare_op=ALU.not_equal, fill=1.0,
                               base=0, pattern=[[-1, 128]], channel_multiplier=1).then_inc(made, 1)
            pool.memset(xn_t[:, :, 0:1], 0.0).then_inc(summed, 2)

            for e in range(E):
                pool.wait_ge(hi_split, e + 1)
                nc.gpsimd.tensor_tensor(w1_lo[:, e, :], w1_raw[:, e, :], as_f32(w1_hi[:, e, :]),
                                        ALU.subtract).then_inc(lo_split, 1)
            for e in range(E):
                h = slice(e * FT, (e + 1) * FT)
                pool.wait_ge(hi_split, E + e + 1)
                nc.gpsimd.tensor_tensor(w2_lo[:, h, :], w2_raw[:, h, :], as_f32(w2_hi[:, h, :]),
                                        ALU.subtract).then_inc(lo_split, 1)
            pool.wait_ge(hi_split, 2 * E + 2)
            nc.gpsimd.tensor_tensor(wo_lo[:, :], wo_raw, as_f32(wo_hi[:, :]), ALU.subtract).then_inc(lo_split, 1)
            nc.gpsimd.tensor_tensor(pj_lo[:, :, :], proj_raw, as_f32(pj_hi[:, :, :]), ALU.subtract).then_inc(lo_split, 1)

            def g_lo_half(s1, gb):
                pool.wait_ge(g_hi_done, 2 * s1 + 2)
                h = slice(FT * BLK // 2, FT * BLK)
                nc.gpsimd.tensor_tensor(g_lo[:, gb, h], g[:, gb, h], as_f32(g_hi[:, gb, h]),
                                        ALU.subtract).then_inc(g_lo_pool, 1)

            def one_pass(i, kind):
                for t in range(8):
                    s = 8 * i + t
                    if not (kind == LAST and t == 7):
                        g_lo_half(s + 1, (t + 1) % 2)
                    if kind == NORMING and (1 if i > 0 else 3) <= t <= 4:
                        pool.wait_ge(rstd_ready, i + 2)
                        if t >= 3:
                            pool.wait_ge(xn_ready, 2 * i + 3)
                        norm_scale(nc.gpsimd, (i + 1) * (2 * BLK), (2 * t - 2, 2 * t - 1))
                    pool.wait_ge(combined, s + 3)
                    pool.wait_ge(summed, s + 2)
                    c = cur[:, ds((s // E % NB) * BLK, BLK)]
                    nc.gpsimd.tensor_tensor(c, c, tmp[:, t % 2, :], ALU.add).then_inc(summed, 1)

            g_lo_half(0, 0)
            passes(pool, one_pass)

        @block.scalar
        def _(act):
            act.dma_start(wg_c[:, :, :], wg.rearrange("d (r e) -> d r e", r=R)).then_inc(gate_loaded, DMA)
            act.dma_start(bg_b[:, :], bg.partition_broadcast(RP)).then_inc(gate_loaded, DMA)
            act.wait_ge(made, 3)
            nc.scalar.activation(th[:, 0, 0:1], ident[:, 0:1], ACT.Gelu_apprx_tanh)

            for e in range(E):
                act.wait_ge(w1_loaded[e], DMA)
                nc.scalar.activation(w1_hi[:, e, :], w1_raw[:, e, :], ACT.Copy).then_inc(hi_split, 1)

            def router_tanh(k):
                act.wait_ge(lgd_ready, k + 1)
                nc.scalar.activation(lg_th[:, :], lg_d[:, :], ACT.Tanh).then_inc(lgth_ready, 1)

            def hidden(s1, e, gb, first=None, between=None):
                if first is not None:
                    first()
                if isinstance(s1, int) and s1 == 0:
                    act.wait_ge(lo_split, E)
                else:
                    act.wait_ge(down_done, s1)
                for half in range(2):
                    for ft in (2 * half, 2 * half + 1):
                        act.wait_ge(up_done, 4 * s1 + ft + 1)
                        nc.scalar.activation(g[:, gb, ft * BLK:(ft + 1) * BLK], hb[ft][:, :], ACT.Gelu_apprx_tanh,
                                             bias=b1_c[:, e * FT + ft:e * FT + ft + 1]).then_inc(gelu_done, 1)
                    act.wait_ge(gelu_done, 4 * s1 + 2 * half + 2)
                    h = slice(half * FT * BLK // 2, (half + 1) * FT * BLK // 2)
                    nc.scalar.activation(g_hi[:, gb, h], g[:, gb, h], ACT.Copy).then_inc(g_hi_done, 1)
                    if half == 0 and between is not None:
                        between()

            def one_pass(i, kind):
                def take_rw():
                    act.wait_ge(p_full, 4 * i + 1)
                    nc.scalar.activation(rw[:, :, :], pb[:, :].rearrange("p (a t) -> p a t", a=2), ACT.Tanh,
                                         scale=0.5).then_inc(p_empty, 1)

                def take_ag():
                    act.wait_ge(p_full, 4 * i + 2)
                    nc.scalar.activation(ag[:, :, :], pb[:, :].rearrange("p (a t) -> p a t", a=2), ACT.Tanh,
                                         scale=0.5).then_inc(p_empty, 1)

                def take_kv():
                    act.wait_ge(p_full, 4 * i + 3)
                    nc.scalar.activation(kv[:, 0, :], pb[:, 0:LEN], ACT.Tanh)
                    nc.scalar.activation(kv[:, 1, :], pb[:, LEN:2 * LEN], ACT.Copy).then_inc(p_empty, 1)

                def take_s():
                    act.wait_ge(p_full, 4 * i + 4)
                    nc.scalar.activation(xn_t[:, ds(i, 1), 1:LEN + 1].rearrange("p a t -> p (a t)"), pb[:, 0:LEN],
                                         ACT.Identity, bias=vec[:, 2:3]).then_inc(p_empty, 1)

                first = {1: take_rw, 2: take_ag, 3: take_kv, 7: take_s}
                between = {2: lambda: router_tanh(2 * i + 1)}
                if kind != LAST:
                    between[6] = lambda: router_tanh(2 * i + 2)
                if kind in (ENDING, LAST):
                    b = 2 * (i - TAIL_PASS)
                    between[0] = lambda: end_tanh(b)
                    between[4] = lambda: end_tanh(b + 1)
                if kind == LAST:
                    between[6] = lambda: end_tanh(NB - 2)
                for t in range(8):
                    if kind == LAST and t == 7:
                        take_s()
                    else:
                        hidden(8 * i + t + 1, (t + 1) % 4, (t + 1) % 2, first.get(t), between.get(t))

            def end_tanh(b):
                act.wait_ge(summed, 2 + STEPS - E * (NB - b - 1))
                if b >= 2:
                    act.wait_ge(z_ready, b - 1)
                nc.scalar.activation(th[:, b % 2, :], cur[:, b * BLK:(b + 1) * BLK], ACT.Tanh,
                                     scale=0.5).then_inc(th_ready, 1)

            act.wait_ge(w2_loaded, DMA)
            for e in range(E):
                h = slice(e * FT, (e + 1) * FT)
                nc.scalar.activation(w2_hi[:, h, :], w2_raw[:, h, :], ACT.Copy).then_inc(hi_split, 1)
            act.wait_ge(mixw_loaded, DMA * MIXW)
            nc.scalar.activation(wo_hi[:, :], wo_raw, ACT.Copy).then_inc(hi_split, 1)
            nc.scalar.activation(pj_hi[:, :, :], proj_raw, ACT.Copy).then_inc(hi_split, 1)
            router_tanh(0)
            act.wait_ge(small_loaded, DMA * SMALL)
            hidden(0, 0, 0)
            act.wait_ge(lo_split, 2 * E)
            passes(act, one_pass)
            end_tanh(NB - 1)

        @block.vector
        def _(dve):
            class Own:
                base, n = 0, 0

            def link(ins):
                Own.n += 1
                ins.then_inc(dve_step, 1)
                dve.wait_ge(dve_step, Own.base + Own.n)

            def inverse_root(v, n, out):
                a, b, t = y0[:, 0:n], y1[:, 0:n], yt[:, 0:n]
                link(nc.vector.tensor_scalar(a.bitcast(i32), v.bitcast(i32), -0.5, RSQRT_SEED, ALU.mult, ALU.add))
                for target in (b, a, out):
                    link(nc.vector.tensor_tensor(t, a, a, ALU.mult))
                    link(nc.vector.scalar_tensor_tensor(out=t, in0=t, scalar=-0.5, in1=v, op0=ALU.mult, op1=ALU.mult))
                    last = nc.vector.scalar_tensor_tensor(out=target, in0=t, scalar=1.5, in1=a, op0=ALU.add, op1=ALU.mult)
                    if target is not out:
                        link(last)
                    a = target
                return last

            def norm_stats(off, loaded=None):
                for t in range(2 * TPB):
                    if loaded is not None and t % TPB == 0:
                        dve.wait_ge(loaded[t // TPB], DMA)
                    last = nc.vector.bn_stats(stats[:, t, :], cur[:, ds(off + t * D, D)])
                link(last)
                mean_a, sq_a, mean_b, sq_b = (stats[:, :, n] for n in (1, 2, 4, 5))
                nc.vector.tensor_tensor(mean[:, :], mean_a, mean_b, ALU.add)
                link(nc.vector.tensor_tensor(mdif[:, :], mean_a, mean_b, ALU.subtract))
                nc.vector.tensor_scalar(mean[:, :], mean[:, :], 0.5, None, ALU.mult)
                nc.vector.tensor_tensor(veps[:, :], sq_a, sq_b, ALU.add)
                link(nc.vector.tensor_tensor(mdif[:, :], mdif[:, :], mdif[:, :], ALU.mult))
                link(nc.vector.tensor_scalar(veps[:, :], veps[:, :], 1.0 / D, LN_EPS, ALU.mult, ALU.add))
                link(nc.vector.scalar_tensor_tensor(out=veps[:, :], in0=mdif[:, :], scalar=0.25, in1=veps[:, :],
                                                    op0=ALU.mult, op1=ALU.add))

            def norm_root():
                inverse_root(veps[:, :], 2 * TPB, rstd[:, :]).then_inc(rstd_ready, 1)

            def store_block(seq, off, job):
                dve.wait_ge(r_full, job + 1)
                dve.wait_ge(summed, 2)
                xb = xn_t[:, ds(seq, 2), 1:LEN + 1]
                nc.vector.tensor_scalar(xb, rb[:, :].rearrange("p (b t) -> p b t", b=2), 1.0, None,
                                        ALU.mult).then_inc(r_empty, 1)
                dve.wait_ge(r_empty, job + 1)
                link(nc.vector.tensor_scalar(cur[:, ds(off, BLK)].rearrange("p (b t) -> p b t", b=2), xb, 1.0, None,
                                             ALU.mult))

            def split_cur(k, q, off, sums, rnd):
                if sums is not None:
                    dve.wait_ge(summed, sums)
                w = as_f32(wg_hl[:, ds(rnd, 1), :]).rearrange("p r c -> p (r c)")
                nc.vector.tensor_scalar(wg_now[:, q, :], w, 1.0, None, ALU.mult)
                nc.vector.tensor_scalar(cur_hi[:, q, :], cur[:, ds(off, BLK)], 1.0, None, ALU.mult).then_inc(cur_split, 1)
                dve.wait_ge(cur_split, 2 * k + 1)
                nc.vector.tensor_tensor(cur_lo[:, q, :], cur[:, ds(off, BLK)], as_f32(cur_hi[:, q, :]),
                                        ALU.subtract).then_inc(cur_split, 1)

            def router_scores(k, job, rnd):
                l3 = lg[:, :].rearrange("p (t e) -> p t e", e=E)
                bg3 = bg_b[:, ds(rnd * E, E)].unsqueeze(1).to_broadcast([RP, RT, E])
                dve.wait_ge(r_full, job + 1)
                nc.vector.transpose(lgt[:, :, :].rearrange("p t c -> p (t c)"), rb[0:RP, :]).then_inc(r_empty, 1)
                dve.wait_ge(r_empty, job + 1)
                link(nc.vector.tensor_tensor(l3, lgt[:, :, 0:E], lgt[:, :, E:2 * E], ALU.add))
                link(nc.vector.tensor_tensor(l3, l3, bg3, ALU.add))
                for e in range(E):
                    if e > 0:
                        last = nc.vector.tensor_tensor(ahead[:, :, e, 0:e], l3[:, :, 0:e],
                                                       l3[:, :, e:e + 1].to_broadcast([RP, RT, e]), ALU.is_ge)
                    if e < E - 1:
                        nc.vector.tensor_tensor(ahead[:, :, e, e + 1:E], l3[:, :, e + 1:E],
                                                l3[:, :, e:e + 1].to_broadcast([RP, RT, E - 1 - e]), ALU.is_gt)
                link(last)
                link(nc.vector.tensor_reduce(rank[:, :], ahead[:, :, :, :].rearrange("p t a b -> p (t a) b"), AX.X, ALU.add))
                nc.vector.tensor_scalar(half_sel[:, :], rank[:, :], 1.5, 0.5, ALU.is_lt, ALU.mult)
                link(nc.vector.scalar_tensor_tensor(out=sel_l[:, :], in0=rank[:, :], scalar=1.5, in1=lg[:, :],
                                                    op0=ALU.is_lt, op1=ALU.mult))
                link(nc.vector.tensor_reduce(sel_sum[:, :], sel_l[:, :].rearrange("p (t e) -> p t e", e=E), AX.X, ALU.add))
                nc.vector.scalar_tensor_tensor(out=lg_d[:, :].rearrange("p (t e) -> p t e", e=E),
                                               in0=sel_sum[:, :].unsqueeze(2).to_broadcast([RP, RT, E]), scalar=-0.5,
                                               in1=l3, op0=ALU.mult, op1=ALU.add).then_inc(lgd_ready, 1)

            def router_gates(k, q):
                dve.wait_ge(lgth_ready, k + 1)
                nc.vector.scalar_tensor_tensor(out=cw[:, q, :], in0=lg_th[:, :], scalar=1.0, in1=half_sel[:, :],
                                               op0=ALU.add, op1=ALU.mult).then_inc(cw_ready, 1)

            def g_lo_half(s1, gb):
                dve.wait_ge(g_hi_done, 2 * s1 + 1)
                h = slice(0, FT * BLK // 2)
                nc.vector.tensor_tensor(g_lo[:, gb, h], g[:, gb, h], as_f32(g_hi[:, gb, h]),
                                        ALU.subtract).then_inc(g_lo_dve, 1)

            def combine(i, t):
                s, q, e = 8 * i + t, t // 4, t % 4
                dve.wait_ge(down_done, s + 2)
                if e == 0:
                    dve.wait_ge(cwb_ready[q], DMA * (i + 1))
                dve.wait_ge(summed, s + 1)
                gates = cw_b[:, q, :].rearrange("p (c t e) -> p e t c", t=RT, e=E)[:, e]
                nc.vector.scalar_tensor_tensor(out=tmp[:, t % 2, :].rearrange("p (t c) -> p t c", t=RT),
                                               in0=yb[t % 2][:, :].rearrange("p (t c) -> p t c", t=RT),
                                               scalar=b2_c[:, e:e + 1], in1=gates,
                                               op0=ALU.add, op1=ALU.mult).then_inc(combined, 1)

            norm_stats(0, x_loaded)
            norm_root()
            dve.wait_ge(rstd_ready, 1)
            norm_scale(nc.vector, 0, range(2 * TPB))
            dve.wait_ge(gate_loaded, DMA * GATEW)
            nc.vector.tensor_scalar(wg_hl[:, :, 0:E], wg_c[:, :, :], 1.0, None, ALU.mult).then_inc(wg_split, 1)
            dve.wait_ge(wg_split, 1)
            nc.vector.tensor_tensor(wg_hl[:, :, E:2 * E], wg_c[:, :, :], as_f32(wg_hl[:, :, 0:E]),
                                    ALU.subtract).then_inc(wg_split, 1)
            dve.wait_ge(wg_split, 2)
            dve.wait_ge(r_full, 1)
            nc.vector.tensor_scalar(cur[:, 0:BLK], rb[:, :], 1.0, None, ALU.mult).then_inc(r_empty, 1)
            dve.wait_ge(r_empty, 1)
            split_cur(0, 0, 0, None, 0)
            dve.wait_ge(summed, 2)
            nc.vector.tensor_scalar(xn_t[:, 0:2, 1:LEN + 1], cur[:, 0:BLK].rearrange("p (b t) -> p b t", b=2), 1.0,
                                    None, ALU.mult)
            dve.wait_ge(made, 3)
            router_scores(0, 1, 0)
            router_gates(0, 0)
            dve.wait_ge(small_loaded, DMA * SMALL)
            nc.vector.tensor_scalar(gnw4[:, :], vec[:, 0:1], 0.25, None, ALU.mult)
            nc.vector.tensor_scalar(gnb2[:, :], vec[:, 1:2], 0.5, None, ALU.mult).then_inc(combined, 2)
            g_lo_half(0, 0)
            store_block(2, BLK, 2)
            split_cur(1, 1, BLK, None, 0)
            for c in range(2, NB):
                dve.wait_ge(x_loaded[c], DMA)

            def mixer_input(i, job, kinds):
                xs = xn_t[:, ds(i, 1), :].rearrange("p a t -> p (a t)")
                if job == 0:
                    link(nc.vector.tensor_tensor(xx[:, :], xs[:, 0:LEN], xs[:, 1:LEN + 1], ALU.subtract))
                else:
                    dve.wait_ge(xm_ready, 6 * i + 2 * job)
                for n, k in enumerate(kinds):
                    last = nc.vector.scalar_tensor_tensor(out=xm[:, n, :], in0=xx[:, :], scalar=mix[:, k:k + 1],
                                                          in1=xs[:, 1:LEN + 1], op0=ALU.mult, op1=ALU.add)
                link(last)
                b = job % 2
                if job == 2:
                    dve.wait_ge(p_full, 4 * i + 1)
                nc.vector.tensor_scalar(xm_hi[:, b, :, :], xm[:, :, :], 1.0, None, ALU.mult).then_inc(xm_ready, 1)
                dve.wait_ge(xm_ready, 6 * i + 2 * job + 1)
                nc.vector.tensor_tensor(xm_lo[:, b, :, :], xm[:, :, :], as_f32(xm_hi[:, b, :, :]),
                                        ALU.subtract).then_inc(xm_ready, 1)

            def mixer_scan(i):
                dve.wait_ge(p_empty, 4 * i + 3)
                nc.vector.tensor_scalar(dec[:, :], rw[:, 1, :], -0.5, 0.5, ALU.mult, ALU.add)
                link(nc.vector.scalar_tensor_tensor(out=uk[:, :], in0=ag[:, 0, :], scalar=1.0, in1=kv[:, 0, :],
                                                    op0=ALU.add, op1=ALU.mult))
                link(nc.vector.scalar_tensor_tensor(out=u[:, :], in0=uk[:, :], scalar=0.5, in1=kv[:, 1, :],
                                                    op0=ALU.mult, op1=ALU.mult))
                link(nc.vector.tensor_tensor_scan(st[:, :], dec[:, :], u[:, :], 0.0, ALU.mult, ALU.add))
                nc.vector.scalar_tensor_tensor(out=mixed[:, :], in0=rw[:, 0, :], scalar=1.0, in1=st[:, :],
                                               op0=ALU.add, op1=ALU.mult).then_inc(m_ready, 1)

            def mixer_norm(i, job):
                dve.wait_ge(r_full, job + 1)
                m3 = rb[:, 0:2 * D].rearrange("p (g c) -> p g c", c=GW)
                link(nc.vector.tensor_reduce(gsum[:, :], m3, AX.X, ALU.add))
                nc.vector.scalar_tensor_tensor(out=cen[:, :].rearrange("p (g c) -> p g c", c=GW),
                                               in0=gsum[:, :].unsqueeze(2).to_broadcast([128, 2 * GRP, GW]),
                                               scalar=-1.0 / GW, in1=m3, op0=ALU.mult, op1=ALU.add).then_inc(r_empty, 1)
                dve.wait_ge(r_empty, job + 1)
                link(nc.vector.tensor_tensor(sq[:, :], cen[:, :], cen[:, :], ALU.mult))
                link(nc.vector.tensor_reduce(gvar[:, :], sq[:, :].rearrange("p (g c) -> p g c", c=GW), AX.X, ALU.add))
                link(nc.vector.tensor_scalar(gvar[:, :], gvar[:, :], 1.0 / (4 * GW), GN_EPS, ALU.mult, ALU.add))
                link(inverse_root(gvar[:, :], 2 * GRP, rt[:, :]))
                nc.vector.tensor_tensor(mn[:, :].rearrange("p (g c) -> p g c", c=GW),
                                        cen[:, :].rearrange("p (g c) -> p g c", c=GW),
                                        rt[:, :].unsqueeze(2).to_broadcast([128, 2 * GRP, GW]),
                                        ALU.mult).then_inc(mn_ready, 1)

            def mixer_gate(i, job):
                dve.wait_ge(r_full, job + 1)
                nc.vector.tensor_scalar(gn[:, :], rb[:, 0:LEN], gnw4[:, :], gnb2[:, :], ALU.mult,
                                        ALU.add).then_inc(r_empty, 1)
                dve.wait_ge(r_empty, job + 1)
                link(nc.vector.scalar_tensor_tensor(out=gated[:, :], in0=ag[:, 1, :], scalar=1.0, in1=gn[:, :],
                                                    op0=ALU.add, op1=ALU.mult))
                nc.vector.tensor_scalar(go_hi[:, :], gated[:, :], 1.0, None, ALU.mult).then_inc(go_ready, 1)
                dve.wait_ge(go_ready, 2 * i + 1)
                nc.vector.tensor_tensor(go_lo[:, :], gated[:, :], as_f32(go_hi[:, :]), ALU.subtract).then_inc(go_ready, 1)

            def end_product(b):
                q = b % 2
                dve.wait_ge(th_ready, b + 1)
                link(nc.vector.scalar_tensor_tensor(out=th[:, q, :], in0=th[:, q, :], scalar=1.0,
                                                    in1=cur[:, b * BLK:(b + 1) * BLK], op0=ALU.add, op1=ALU.mult))
                nc.vector.scalar_tensor_tensor(out=z[:, q, :].rearrange("p (b t) -> p b t", b=2),
                                               in0=th[:, q, :].rearrange("p (b t) -> p b t", b=2), scalar=0.5,
                                               in1=xn_t[:, 2 * b:2 * b + 2, 1:LEN + 1], op0=ALU.mult,
                                               op1=ALU.mult).then_inc(z_ready, 1)

            def end_output(b, job):
                q = b % 2
                dve.wait_ge(r_full, job + 1)
                dve.wait_ge(x_again[q], DMA * (b // 2 + 1))
                if b >= 2:
                    dve.wait_ge(stored[q], DMA * (b // 2))
                nc.vector.tensor_tensor(o[:, q, :], rb[:, :], xr[:, q, :], ALU.add).then_inc(r_empty, 1)

            def one_pass(i, kind):
                Own.n = 0
                job = jobs_of(i, kind)
                b = 2 * (i - TAIL_PASS)
                for t in range(8):
                    s = 8 * i + t
                    if t == 0:
                        mixer_input(i, 0, (P_R, P_W))
                        if kind == NORMING and i == 0:
                            norm_stats(2 * BLK)
                        elif kind == NORMING:
                            norm_root()
                    elif t == 1:
                        mixer_input(i, 1, (P_A, P_G))
                        if kind in (ENDING, LAST):
                            end_product(b)
                    elif t == 2:
                        mixer_input(i, 2, (P_K, P_V))
                        if kind == NORMING and i == 0:
                            norm_root()
                            dve.wait_ge(rstd_ready, 2)
                            norm_scale(nc.vector, 2 * BLK, range(TPB))
                    elif t == 3:
                        if kind in (ENDING, LAST):
                            end_output(b, job["end_even"])
                        mixer_scan(i)
                        if kind == NORMING:
                            store_block(4 * i + 4, i * (2 * BLK) + 2 * BLK, job["norm_even"])
                        if kind != LAST:
                            split_cur(2 * i + 2, 0, ((i + 1) % 4) * (2 * BLK), None if kind == NORMING else 8 * i - 18,
                                      (i + 1) // 4)
                    elif t == 4:
                        mixer_norm(i, job["mixed"])
                    elif t == 5:
                        if kind in (ENDING, LAST):
                            end_product(b + 1)
                    elif t == 6:
                        mixer_gate(i, job["mn"])
                        if kind == NORMING and i + 1 < SPLIT_PASSES:
                            dve.wait_ge(xn_ready, 2 * i + 4)
                            norm_stats((i + 2) * (2 * BLK))
                    elif t == 7:
                        if kind == NORMING:
                            store_block(4 * i + 6, i * (2 * BLK) + 3 * BLK, job["norm_odd"])
                        if kind in (ENDING, LAST):
                            end_output(b + 1, job["end_odd"])
                        if kind == LAST:
                            end_product(NB - 2)
                        else:
                            split_cur(2 * i + 3, 1, ((i + 1) % 4) * (2 * BLK) + BLK,
                                      None if kind == NORMING else 8 * i - 14, (i + 1) // 4)
                    if not (kind == LAST and t == 7):
                        g_lo_half(s + 1, (t + 1) % 2)
                    if t == 1:
                        router_scores(2 * i + 1, job["logits_odd"], i // 4)
                    elif t == 2:
                        router_gates(2 * i + 1, 1)
                    elif t == 5 and kind != LAST:
                        router_scores(2 * i + 2, job["logits_even"], (i + 1) // 4)
                    elif t == 6 and kind != LAST:
                        router_gates(2 * i + 2, 0)
                    combine(i, t)

            ROUTER, INPUT, SCAN, NORM, GATE = 6, 4, 3, 14, 1
            LINKS = 2 * ROUTER + INPUT + SCAN + NORM + GATE

            Own.base, Own.n = Own.base + Own.n, 0
            for i in range(SPLIT_PASSES):
                one_pass(i, NORMING)
                Own.base, Own.n = Own.base + Own.n, 0
            first = Own.base
            with dve.Fori(SPLIT_PASSES, TAIL_PASS) as i:
                Own.base = first - LINKS * SPLIT_PASSES + LINKS * i
                one_pass(i, PLAIN)
                assert Own.n == LINKS, Own.n
            Own.base = first + LINKS * (TAIL_PASS - SPLIT_PASSES)
            for i in range(TAIL_PASS, PASSES):
                one_pass(i, LAST if i == PASSES - 1 else ENDING)
                Own.base, Own.n = Own.base + Own.n, 0

            end_output(NB - 2, end_job(NB - 2))
            dve.wait_ge(p_empty, 4 * PASSES)
            end_product(NB - 1)
            end_output(NB - 1, end_job(NB - 1))

        @block.tensor
        def _(pe):
            def mm3(out_ap, w_hi, w_lo, v_hi, v_lo, start=True, stop=True):
                nc.tensor.matmul(out_ap, w_hi, v_lo, start=start, stop=False)
                nc.tensor.matmul(out_ap, w_lo, v_hi, start=False, stop=False)
                return nc.tensor.matmul(out_ap, w_hi, v_hi, start=False, stop=stop)

            def turn(job, src, tiles, ready, count, first=False):
                pe.wait_ge(ready, count)
                if not first:
                    pe.wait_ge(r_empty, job)
                for t in range(tiles):
                    ins = nc.tensor.transpose(rb[:, t * D:(t + 1) * D], src[:, t * D:(t + 1) * D], ident[:, :])
                    if first and t == 0:
                        ins.then_inc(down_done, 1)
                ins.then_inc(r_full, 1)

            def up(s1, e, q, split):
                first = isinstance(s1, int) and s1 == 0
                if split is not None:
                    pe.wait_ge(cur_split, split)
                for ft in range(FT):
                    if not first:
                        pe.wait_ge(gelu_done, 4 * s1 + ft - 3)
                    w = slice(ft * D, (ft + 1) * D)
                    mm3(hb[ft][:, :], w1_hi[:, e, w], w1_lo[:, e, w], cur_hi[:, q, :], cur_lo[:, q, :]).then_inc(up_done, 1)

            def down(s, e, b):
                pe.wait_ge(combined, s + 1)
                for ft in range(FT):
                    if ft % 2 == 0:
                        pe.wait_ge(g_hi_done, 2 * s + ft // 2 + 1)
                    hi = g_hi[:, b, ft * BLK:(ft + 1) * BLK]
                    nc.tensor.matmul(yb[b][:, :], w2_hi[:, e * FT + ft, :], hi, start=(ft == 0), stop=False)
                    nc.tensor.matmul(yb[b][:, :], w2_lo[:, e * FT + ft, :], hi, start=False, stop=False)
                for ft in range(FT):
                    if ft == 0:
                        pe.wait_ge(g_lo_dve, s + 1)
                    if ft == FT // 2:
                        pe.wait_ge(g_lo_pool, s + 1)
                    last = nc.tensor.matmul(yb[b][:, :], w2_hi[:, e * FT + ft, :], g_lo[:, b, ft * BLK:(ft + 1) * BLK],
                                            start=False, stop=(ft == FT - 1))
                last.then_inc(down_done, 1)

            def logits(k, q, job):
                pe.wait_ge(cur_split, 2 * (k + 1))
                pe.wait_ge(r_empty, job)
                w = wg_now[:, q, :]
                nc.tensor.matmul(rb[0:2 * E, :], w, cur_lo[:, q, :], start=True, stop=False)
                nc.tensor.matmul(rb[0:2 * E, :], w, cur_hi[:, q, :], start=False, stop=True).then_inc(r_full, 1)

            def project(i, job, kinds):
                pe.wait_ge(xm_ready, 6 * i + 2 * job + 2)
                if job > 0:
                    pe.wait_ge(p_empty, 4 * i + job)
                for n, k in enumerate(kinds):
                    last = mm3(pb[:, n * LEN:(n + 1) * LEN], pj_hi[:, k, :], pj_lo[:, k, :],
                               xm_hi[:, job % 2, n, :], xm_lo[:, job % 2, n, :])
                last.then_inc(p_full, 1)

            def one_pass(i, kind):
                job = jobs_of(i, kind)
                b = 2 * (i - TAIL_PASS)
                for t in range(8):
                    if not (kind == LAST and t == 7):
                        k1 = (t + 1) // 4
                        up(8 * i + t + 1, (t + 1) % 4, k1 % 2, 2 * (2 * i + k1 + 1) if (t + 1) % 4 == 0 else None)
                    if kind == NORMING and t == 3:
                        turn(job["norm_even"], xn_st[:, 0, :], TPB, xn_ready, 2 * i + 3)
                    if kind == NORMING and t == 7:
                        turn(job["norm_odd"], xn_st[:, 1, :], TPB, xn_ready, 2 * i + 4)
                    down(8 * i + t, t % 4, t % 2)
                    if t == 0:
                        logits(2 * i + 1, 1, job["logits_odd"])
                        project(i, 0, (P_R, P_W))
                    elif t == 1:
                        project(i, 1, (P_A, P_G))
                    elif t == 2:
                        project(i, 2, (P_K, P_V))
                        if kind in (ENDING, LAST):
                            turn(job["end_even"], z[:, 0, :], TPB, z_ready, b + 1)
                    elif t == 3:
                        turn(job["mixed"], mixed, 2, m_ready, i + 1)
                    elif t == 4 and kind != LAST:
                        logits(2 * i + 2, 0, job["logits_even"])
                    elif t == 5:
                        turn(job["mn"], mn, 2, mn_ready, i + 1)
                    elif t == 6:
                        pe.wait_ge(go_ready, 2 * i + 2)
                        pe.wait_ge(p_empty, 4 * i + 3)
                        mm3(pb[:, 0:LEN], wo_hi[:, :], wo_lo[:, :], go_hi[:, :], go_lo[:, :]).then_inc(p_full, 1)
                        if kind in (ENDING, LAST):
                            turn(job["end_odd"], z[:, 1, :], TPB, z_ready, b + 2)
                    elif t == 7 and kind == LAST:
                        turn(job["end_6"], z[:, 0, :], TPB, z_ready, NB - 1)

            pe.wait_ge(made, 3)
            for _ in range(WARM_UP):
                nc.tensor.transpose(pb[:, 0:D], ident[:, :], ident[:, :])
            turn(0, xn_st[:, 0, :], TPB, xn_ready, 1, first=True)
            logits(0, 0, 1)
            pe.wait_ge(lo_split, 1)
            up(0, 0, 0, 2)
            turn(2, xn_st[:, 1, :], TPB, xn_ready, 2)
            pe.wait_ge(lo_split, 2 * E + 2)
            passes(pe, one_pass)
            turn(end_job(NB - 1), z[:, 1, :], TPB, z_ready, NB)


def kernel(**inputs):
    import concourse.bacc as _bacc
    from concourse.bass_utils import run_bass_kernel_spmd as _run

    a = {k: np.asarray(v) for k, v in inputs.items()}
    kinds = "rwkvag"
    host = {
        "x": a["L0_attn_x"].reshape(TOK, D),
        "proj_t": np.concatenate([a[f"L0_attn_W_{k}"].T for k in kinds], axis=1),
        "mixes": np.stack([a[f"L0_attn_x_{k}"].reshape(D) for k in kinds], axis=1),
        "wout_t": a["L0_attn_W_out"].T,
        "chan_vecs": np.stack([a["L0_attn_gn_w"], a["L0_attn_gn_b"], a["L0_attn_b_out"]], axis=1),
        "wg": a["L0_ffn_Wg"].transpose(1, 0, 2).reshape(D, R * E),
        "bg": a["L0_ffn_bg"].reshape(R * E),
        "w1": a["L0_ffn_W1"],
        "b1": a["L0_ffn_b1"].reshape(E * FT, D).T,
        "w2": a["L0_ffn_W2"],
        "b2": a["L0_ffn_b2"].T,
    }
    nc = _bacc.Bacc("TRN2", target_bir_lowering=False, num_devices=1)
    arrays, args = {}, []
    for name, v in host.items():
        v = np.ascontiguousarray(v)
        arrays[f"in_{name}"] = v
        args.append(nc.dram_tensor(f"in_{name}", v.shape, mybir.dt.from_np(v.dtype), kind="ExternalInput").ap())
    scratch = nc.dram_tensor("cw_scratch", (2, RP, RT * E), mybir.dt.float32, kind="Internal").ap()
    out = nc.dram_tensor("out_0", (TOK, D), mybir.dt.float32, kind="ExternalOutput").ap()
    mixer_gated_experts(nc, *args, scratch, out)
    r = _run(nc, [arrays], core_ids=[0])
    return r.results[0]["out_0"].reshape(SEQS, LEN, D)
```
